# Optimizing a Trainium2 kernel written in Bass

```python
import numpy as np
import jax
import jax.numpy as jnp

def _softmax(x, axis=-1):
    return jax.nn.softmax(x, axis=axis)

def _gelu(x):
    return jax.nn.gelu(x, approximate=True)

def _silu(x):
    return jax.nn.silu(x)

def _sigmoid(x):
    return jax.nn.sigmoid(x)

def _layernorm(x, axis=-1, eps=1e-05):
    m = jnp.mean(x, axis=axis, keepdims=True)
    v = jnp.var(x, axis=axis, keepdims=True)
    return (x - m) / jnp.sqrt(v + eps)

def _scatter_add(tgt, idx, src, axis=0):
    return tgt.at[idx].add(src)

def _segment_sum(src, seg, n):
    return jax.ops.segment_sum(src, seg, n)
kernel_name = 'mk_xattn_seq_d1_seqx_r2_f7251e'

def setup_inputs(seed: int=0):
    np.random.seed(seed)
    _w = jnp.asarray

    def _rec_inputs():
        import jax
        import jax.numpy as jnp
        _rk = jax.random.key(seed)
        x = -0.000125 + 0.9999 * jax.random.normal(jax.random.fold_in(_rk, 1), (8, 512, 1024), jnp.float32)
        _lenS = 512 - jax.random.randint(jax.random.fold_in(_rk, 7), (8,), 0, max(1, 512 // 4) + 1, jnp.int32)
        _lenS2 = 512 - jax.random.randint(jax.random.fold_in(_rk, 8), (8,), 0, max(1, 512 // 4) + 1, jnp.int32)
        _ctx_2048P = jax.random.normal(jax.random.fold_in(_rk, 11), (8, 16, 1024), jnp.float32)
        _ctx_2048c = jax.random.dirichlet(jax.random.fold_in(_rk, 511), 0.3 * jnp.ones((16,), jnp.float32), (8, 512))
        _ctx_2048t = jnp.einsum('bsk,bkd->bsd', _ctx_2048c, _ctx_2048P)
        _ctx_2048t = _ctx_2048t * jax.lax.rsqrt(jnp.mean(jnp.square(_ctx_2048t)) + 1e-12) * 0.953939
        ctx_2048 = -1.52775e-05 + 0.999936 * (_ctx_2048t + 0.3 * jax.random.normal(jax.random.fold_in(_rk, 611), (8, 512, 1024), jnp.float32))
        return (x, ctx_2048)
    x, ctx_2048 = _rec_inputs()

    def _L0_xattn_setup():
        import jax, jax.numpy as jnp
        import numpy as np
        B, C, CI, N = (16, 512, 256, 1024)
        EPS = 1e-05

        def _conv1x1(w, b, x):
            return jnp.einsum('oc,bcn->bon', w, x) + b[None, :, None]
        key = jax.random.key(seed)
        ks = jax.random.split(key, 14)
        s = 0.02
        return {'x': jax.random.normal(ks[0], (B, C, N), jnp.float32), 'x_2': jax.random.normal(ks[1], (B, C, N), jnp.float32), 'theta_w': jax.random.normal(ks[2], (CI, C), jnp.float32) * s, 'theta_b': jax.random.normal(ks[3], (CI,), jnp.float32) * s, 'phi_w': jax.random.normal(ks[4], (CI, C), jnp.float32) * s, 'phi_b': jax.random.normal(ks[5], (CI,), jnp.float32) * s, 'g_w': jax.random.normal(ks[6], (CI, C), jnp.float32) * s, 'g_b': jax.random.normal(ks[7], (CI,), jnp.float32) * s, 'w_w': jax.random.normal(ks[8], (C, CI), jnp.float32) * s, 'w_b': jax.random.normal(ks[9], (C,), jnp.float32) * s, 'bn_gamma': jax.random.normal(ks[10], (C,), jnp.float32), 'bn_beta': jax.random.normal(ks[11], (C,), jnp.float32), 'bn_mean': jax.random.normal(ks[12], (C,), jnp.float32), 'bn_var': jax.random.uniform(ks[13], (C,), jnp.float32, 0.5, 1.5)}
    _L0_xattn_all = _L0_xattn_setup()
    _L0_xattn_in = {k: v for k, v in _L0_xattn_all.items() if k in ('theta_w', 'theta_b', 'phi_w', 'phi_b', 'g_w', 'g_b', 'w_w', 'w_b', 'bn_gamma', 'bn_beta', 'bn_mean', 'bn_var')}
    del _L0_xattn_all
    return {'x': x, 'ctx_2048': ctx_2048, 'L0_xattn_theta_w': _L0_xattn_in['theta_w'], 'L0_xattn_theta_b': _L0_xattn_in['theta_b'], 'L0_xattn_phi_w': _L0_xattn_in['phi_w'], 'L0_xattn_phi_b': _L0_xattn_in['phi_b'], 'L0_xattn_g_w': _L0_xattn_in['g_w'], 'L0_xattn_g_b': _L0_xattn_in['g_b'], 'L0_xattn_w_w': _L0_xattn_in['w_w'], 'L0_xattn_w_b': _L0_xattn_in['w_b'], 'L0_xattn_bn_gamma': _L0_xattn_in['bn_gamma'], 'L0_xattn_bn_beta': _L0_xattn_in['bn_beta'], 'L0_xattn_bn_mean': _L0_xattn_in['bn_mean'], 'L0_xattn_bn_var': _L0_xattn_in['bn_var']}

def reference(x, ctx_2048, L0_xattn_theta_w, L0_xattn_theta_b, L0_xattn_phi_w, L0_xattn_phi_b, L0_xattn_g_w, L0_xattn_g_b, L0_xattn_w_w, L0_xattn_w_b, L0_xattn_bn_gamma, L0_xattn_bn_beta, L0_xattn_bn_mean, L0_xattn_bn_var):
    import jax
    import jax.numpy as jnp

    def _L0_xattn_ref(x, x_2, theta_w, theta_b, phi_w, phi_b, g_w, g_b, w_w, w_b, bn_gamma, bn_beta, bn_mean, bn_var):
        import jax, jax.numpy as jnp
        import numpy as np
        B, C, CI, N = (16, 512, 256, 1024)
        EPS = 1e-05

        def _conv1x1(w, b, x):
            return jnp.einsum('oc,bcn->bon', w, x) + b[None, :, None]
        g_x = _conv1x1(g_w, g_b, x_2).transpose(0, 2, 1)
        theta_x = _conv1x1(theta_w, theta_b, x).transpose(0, 2, 1)
        phi_x = _conv1x1(phi_w, phi_b, x_2)
        W = jnp.einsum('bnc,bcm->bnm', theta_x, phi_x) / phi_x.shape[-1]
        y = jnp.einsum('bnm,bmc->bnc', W, g_x).transpose(0, 2, 1)
        wy = _conv1x1(w_w, w_b, y)
        inv_std = jax.lax.rsqrt(bn_var + EPS)
        wy = bn_gamma[None, :, None] * (wy - bn_mean[None, :, None]) * inv_std[None, :, None] + bn_beta[None, :, None]
        return wy + x
    x = _L0_xattn_ref(x, ctx_2048, L0_xattn_theta_w, L0_xattn_theta_b, L0_xattn_phi_w, L0_xattn_phi_b, L0_xattn_g_w, L0_xattn_g_b, L0_xattn_w_w, L0_xattn_w_b, L0_xattn_bn_gamma, L0_xattn_bn_beta, L0_xattn_bn_mean, L0_xattn_bn_var)
    return x

_drawn_inputs = setup_inputs


def setup_inputs(seed=0):
    import zlib

    import numpy as np

    out = dict(_drawn_inputs(seed))
    spreads = {}
    factors = {'L0_xattn_theta_b': 8.0, 'L0_xattn_phi_b': 8.0, 'L0_xattn_g_b': 8.0, 'L0_xattn_w_b': 4.83}
    for name, (base, spread) in spreads.items():
        noise = np.random.default_rng([zlib.crc32(name.encode()), seed]).standard_normal(out[name].shape)
        drawn = base * np.exp(spread * noise) if base else spread * noise
        out[name] = jnp.asarray(drawn.astype(out[name].dtype))
    for name, factor in factors.items():
        out[name] = (out[name] * factor).astype(out[name].dtype)
    return out
```

```python
from contextlib import ExitStack

import concourse.bass as bass
from concourse import mybir

P = 128
BANKS = 8
BANK = 512


def xattn(nc, x, ctx_in, theta_wT, phi_wT, g_w, w_wT, columns, rows, out):
    f32 = mybir.dt.float32
    f32r = mybir.dt.float32r
    bf16 = mybir.dt.bfloat16
    ALU = mybir.AluOpType
    ACT = mybir.ActivationFunctionType

    B, C, N = x.shape
    CI = theta_wT.shape[1]
    CB, IB, NB = C // P, CI // P, N // P
    NH = N // BANK
    EPS = 1e-5
    SLOTS = 4

    THETA_B, PHI_B, G_B = 0, IB, 2 * IB
    W_B, MEAN, BETA, GAMMA, VAR = (3 * IB + n * CB for n in range(5))
    COLS = columns.shape[1]

    TASKS = (["S0", "S1", "S2", "S3", "theta0", "mirror0", "mirror1", "theta1"]
             + ["T3", "T2", "T1", "T0", "L0", "L1", "theta2", "theta3"])
    OUTS = CB * NH
    for n in range(NB):
        TASKS += [f"next{n}", f"out{n}"]
    LAST_TASKS = TASKS[:16] + [f"out{n}" for n in range(OUTS)]
    PER_BATCH = len(TASKS)

    def done(b, task, last=False):
        return PER_BATCH * b + NB + (LAST_TASKS if last else TASKS).index(task) + 1

    def reusable(b, task, last=False):
        return done(b, task, last) - BANKS

    def bank_of(task, last=False):
        return (LAST_TASKS if last else TASKS).index(task) % BANKS

    with ExitStack() as ctx:
        def sb(name, shape, dt=f32):
            return ctx.enter_context(nc.sbuf_tensor(name, shape, dt))

        def sem(name):
            return ctx.enter_context(nc.semaphore(name))

        Z = sb("Z", [P, CB, N])
        X = sb("X", [P, CB, N])
        XH, XL = sb("XH", [P, CB, N], f32r), sb("XL", [P, CB, N], f32r)
        ZTH, ZTL = sb("ZTH", [P, NB, C], f32r), sb("ZTL", [P, NB, C], f32r)
        full = sb("full", [P, CB, C])
        SH, SL = sb("SH", [P, CB, C], f32r), sb("SL", [P, CB, C], f32r)
        thH, thL = sb("thH", [P, IB, N], f32r), sb("thL", [P, IB, N], f32r)
        TH, TL = sb("TH", [P, CB, CI], f32r), sb("TL", [P, CB, CI], f32r)
        LH, LL = sb("LH", [P, IB, C], f32r), sb("LL", [P, IB, C], f32r)
        stage = sb("stage", [P, SLOTS, BANK])
        phiT = sb("phiT", [P, CB, CI])
        phiTH, phiTL = sb("phiTH", [P, CB, CI], f32r), sb("phiTL", [P, CB, CI], f32r)
        thetaTH, thetaTL = sb("thetaTH", [P, CB, CI], f32r), sb("thetaTL", [P, CB, CI], f32r)
        VH, VL = sb("VH", [P, CB, C], f32r), sb("VL", [P, CB, C], f32r)
        cols = sb("cols", [P, COLS])
        phi_b_row = sb("phi_b_row", [P, CI])
        h_row = sb("h_row", [P, C])
        A_row = sb("A_row", [P, C])
        ident = sb("ident", [P, P])
        ones = sb("ones", [P, P])
        unread = sb("unread", [P, N], bf16)
        zsum = sb("zsum", [P, CB])
        phi_sum_parts = sb("phi_sum_parts", [P, CI])
        phi_sum = sb("phi_sum", [P, IB])
        shift = sb("shift", [P, CB])
        a_col = sb("a_col", [P, 4, CB])

        T_full = full[:, 0:2, :].rearrange("p a (b i) -> p (a b) i", i=CI)
        L_full = full[:, 2:4, :]
        gw_raw, wwT_raw = stage[:, 0:IB, :], stage[:, IB:2 * IB, :]
        V_full = full
        thetaT_raw = X[:, 2, :].rearrange("p (a i) -> p a i", i=CI)
        gamma_row, var_row = X[:, 3, 0:C], X[:, 3, C:2 * C]
        newton_a, newton_b = X[:, 1, 0:C], X[:, 1, C:2 * C]
        gb_wide = X[:, 0, 0:IB * P].rearrange("p (a i) -> p a i", i=P)

        bank = [ctx.enter_context(nc.psum_tensor(f"bank{i}", [P, BANK], f32)) for i in range(BANKS)]

        params_loaded = sem("params_loaded")
        rows_loaded = sem("rows_loaded")
        thetaT_loaded = sem("thetaT_loaded")
        phiT_loaded = sem("phiT_loaded")
        slot_moved = [sem(f"slot_moved{i}") for i in range(SLOTS)]
        z_loaded = [sem(f"z_loaded{j}") for j in range(CB)]
        x_loaded = [sem(f"x_loaded{j}") for j in range(CB)]
        ident_zeroed, ident_made = sem("ident_zeroed"), sem("ident_made")
        var_eps, rooted = sem("var_eps"), sem("rooted")
        chained = sem("chained")
        consts_made = sem("consts_made")
        v_filled, v_scaled, v_rounded, v_split = sem("v_filled"), sem("v_scaled"), sem("v_rounded"), sem("v_split")
        w_rounded, w_split = sem("w_rounded"), sem("w_split")
        filled, drained = sem("filled"), sem("drained")
        z_summed = sem("z_summed")
        parts_step, parts_made, phi_summed = sem("parts_step"), sem("parts_made"), sem("phi_summed")
        zt_rounded, x_rounded, s_rounded = sem("zt_rounded"), sem("x_rounded"), sem("s_rounded")
        mirror_rounded, theta_rounded = sem("mirror_rounded"), sem("theta_rounded")
        x_split = sem("x_split")
        t_rounded, t_split = sem("t_rounded"), sem("t_split")
        l_rounded, l_split = sem("l_rounded"), sem("l_split")

        PARTS = ((0, 0), (0, 1), (1, 0))
        ZT, XX, SS, TH_, TT, LLT = (ZTH, ZTL), (XH, XL), (SH, SL), (thH, thL), (TH, TL), (LH, LL)
        THETA_W, PHI_W, VV = (thetaTH, thetaTL), (phiTH, phiTL), (VH, VL)

        block = ctx.enter_context(nc.Block())

        @block.sync
        def _(sp):
            def load_z(b):
                for j in range(CB):
                    sp.dma_start(Z[:, j, :], ctx_in[b, j * P:(j + 1) * P, :]).then_inc(z_loaded[j], 16)

            def load_x(b, j):
                sp.dma_start(X[:, j, :], x[b, j * P:(j + 1) * P, :]).then_inc(x_loaded[j], 16)

            def store(b, n):
                j, h = n // NH, n % NH
                sp.dma_start(out[b, j * P:(j + 1) * P, h * BANK:(h + 1) * BANK],
                             stage[:, n % SLOTS, :]).then_inc(slot_moved[n % SLOTS], 16)

            for m in range(IB):
                sp.dma_start(gw_raw[:, m, :], g_w[m * P:(m + 1) * P, :]).then_inc(slot_moved[m], 16)
                sp.dma_start(wwT_raw[:, m, :], w_wT[m * P:(m + 1) * P, :]).then_inc(slot_moved[IB + m], 16)
            sp.dma_start(cols[:, :], columns).then_inc(params_loaded, 16)
            sp.dma_start(phi_b_row[:, :], rows[0:1, 0:CI].to_broadcast([P, CI])).then_inc(params_loaded, 16)
            sp.dma_start(X[:, 3, :], rows[0:1, CI:CI + 2 * C].to_broadcast([P, 2 * C])).then_inc(rows_loaded, 16)
            load_z(0)
            sp.dma_start(thetaT_raw, theta_wT.rearrange("(a p) i -> p a i", p=P)).then_inc(thetaT_loaded, 16)
            sp.dma_start(phiT[:, :, :], phi_wT.rearrange("(a p) i -> p a i", p=P)).then_inc(phiT_loaded, 16)
            sp.wait_ge(v_scaled, CB + 1)
            load_x(0, 0)
            load_x(0, 1)
            load_x(0, 3)
            sp.wait_ge(w_split, 1)
            load_x(0, 2)

            with sp.Fori(0, B - 1) as b:
                sp.wait_ge(filled, PER_BATCH * b + NB)
                sp.wait_ge(z_summed, CB * b + CB)
                load_z(b + 1)
                for n in range(OUTS):
                    sp.wait_ge(drained, done(b, f"out{n}"))
                    store(b, n)
                    if n % NH == NH - 1:
                        load_x(b + 1, n // NH)
            for n in range(OUTS):
                sp.wait_ge(drained, done(B - 1, f"out{n}", True))
                store(B - 1, n)
            for i in range(SLOTS):
                sp.wait_ge(slot_moved[i], 16 * (1 + B * OUTS // SLOTS))

        @block.gpsimd
        def _(pool):
            nc.gpsimd.memset(ones[:, :], 1.0).then_inc(ident_made, 1)
            nc.gpsimd.memset(ident[:, :], 0.0).then_inc(ident_zeroed, 1)
            pool.wait_ge(ident_zeroed, 1)
            nc.gpsimd.affine_select(out=ident[:, :], in_=ident[:, :], compare_op=ALU.not_equal, fill=1.0, base=0,
                                    pattern=[[-1, P]], channel_multiplier=1).then_inc(ident_made, 1)

        @block.scalar
        def _(act):
            def round_zt(b, n, bk, filled_at):
                act.wait_ge(filled, filled_at)
                nc.scalar.copy(ZTH[:, n, :], bk[:, :]).then_inc(zt_rounded, 1)

            def round_x(b, j):
                act.wait_ge(x_loaded[j], 16 * b + 16)
                nc.scalar.copy(XH[:, j, :], X[:, j, :]).then_inc(x_rounded, 1)

            def round_s(b, i, last):
                act.wait_ge(filled, done(b, f"S{i}", last))
                bk = bank[bank_of(f"S{i}")]
                if i < CB - 1:
                    nc.scalar.copy(full[:, i, (i + 1) * P:C], bk[:, (i + 1) * P:C])
                nc.scalar.copy(SH[:, i, i * P:C], bk[:, i * P:C]).then_inc(s_rounded, 1)

            def round_theta(b, n, last):
                m, h = n % IB, n // IB
                act.wait_ge(filled, done(b, f"theta{n}", last))
                nc.scalar.activation(thH[:, m, h * BANK:(h + 1) * BANK], bank[bank_of(f"theta{n}")][:, :],
                                     ACT.Identity, bias=cols[:, THETA_B + m:THETA_B + m + 1]).then_inc(theta_rounded, 1)

            def batch(b, last):
                for j in range(CB):
                    act.wait_ge(z_loaded[j], 16 * b + 16)
                    if j > 0:
                        act.wait_ge(z_summed, CB * b + j)
                    nc.scalar.activation(unread[:, :], Z[:, j, :], ACT.Copy,
                                         accum_out=zsum[:, j:j + 1]).then_inc(z_summed, 1)
                round_s(b, 0, last)
                round_x(b, 0)
                round_x(b, 1)
                round_s(b, 1, last)
                round_x(b, 2)
                round_x(b, 3)
                round_s(b, 2, last)
                round_s(b, 3, last)
                round_theta(b, 0, last)
                act.wait_ge(filled, done(b, "mirror0", last))
                nc.scalar.copy(SH[:, 1:4, 0:P], bank[bank_of("mirror0")][:, 0:3 * P].rearrange("p (a c) -> p a c", c=P)
                               ).then_inc(mirror_rounded, 1)
                act.wait_ge(filled, done(b, "mirror1", last))
                nc.scalar.copy(SH[:, 2:4, P:2 * P], bank[bank_of("mirror1")][:, 0:2 * P].rearrange("p (a c) -> p a c", c=P))
                nc.scalar.copy(SH[:, 3, 2 * P:3 * P], bank[bank_of("mirror1")][:, 2 * P:3 * P]).then_inc(mirror_rounded, 1)
                round_theta(b, 1, last)
                for n, i in enumerate((3, 2, 1, 0)):
                    act.wait_ge(drained, done(b, f"T{i}", last))
                    nc.scalar.copy(TH[:, i, :], T_full[:, i, :]).then_inc(t_rounded, 1)
                for m in range(IB):
                    act.wait_ge(drained, done(b, f"L{m}", last))
                    nc.scalar.copy(LH[:, m, :], L_full[:, m, :]).then_inc(l_rounded, 1)
                round_theta(b, 2, last)
                round_theta(b, 3, last)
                if not last:
                    for n in range(NB):
                        round_zt(b, n, bank[bank_of(f"next{n}")], done(b, f"next{n}"))

            act.wait_ge(var_eps, 2)
            nc.scalar.activation(newton_a, var_row, ACT.Sqrt).then_inc(rooted, 1)
            nc.scalar.activation(a_col[:, 1, :], a_col[:, 0, :], ACT.Sqrt).then_inc(rooted, 1)
            for n in range(NB):
                round_zt(0, n, bank[n], n + 1)
            act.wait_ge(thetaT_loaded, 16)
            nc.scalar.copy(thetaTH[:, :, :], thetaT_raw).then_inc(w_rounded, 1)
            act.wait_ge(phiT_loaded, 16)
            nc.scalar.copy(phiTH[:, :, :], phiT[:, :, :]).then_inc(w_rounded, 1)
            act.wait_ge(v_scaled, CB)
            nc.scalar.copy(VH[:, :, :], V_full[:, :, :]).then_inc(v_rounded, 1)
            act.wait_ge(v_split, 1)
            with act.Fori(0, B - 1) as b:
                batch(b, False)
            batch(B - 1, True)

        @block.vector
        def _(dve):
            links = [0]

            def link(instruction):
                links[0] += 1
                instruction.then_inc(chained, 1)
                dve.wait_ge(chained, links[0])

            def low(dst, whole, high):
                return nc.vector.tensor_tensor(dst, whole, high.bitcast(f32), ALU.subtract)

            def split_x(b, j):
                dve.wait_ge(x_rounded, CB * b + j + 1)
                low(XL[:, j, :], X[:, j, :], XH[:, j, :]).then_inc(x_split, 1)

            def split_s(b, i):
                dve.wait_ge(s_rounded, CB * b + i + 1)
                low(SL[:, i, i * P:C], bank[bank_of(f"S{i}")][:, i * P:C], SH[:, i, i * P:C]).then_inc(drained, 1)

            def split_theta(b, n):
                m, h = n % IB, n // IB
                part = slice(h * BANK, (h + 1) * BANK)
                dve.wait_ge(theta_rounded, IB * NH * b + n + 1)
                nc.vector.scalar_tensor_tensor(out=thL[:, m, part], in0=bank[bank_of(f"theta{n}")][:, :],
                                               scalar=cols[:, THETA_B + m:THETA_B + m + 1],
                                               in1=thH[:, m, part].bitcast(f32),
                                               op0=ALU.add, op1=ALU.subtract).then_inc(drained, 1)

            def split_zt(rounded_at, n, bk):
                dve.wait_ge(zt_rounded, rounded_at)
                low(ZTL[:, n, :], bk[:, :], ZTH[:, n, :]).then_inc(drained, 1)

            def whole_t(b, i, last):
                dve.wait_ge(filled, done(b, f"T{i}", last))
                nc.vector.scalar_tensor_tensor(out=T_full[:, i, :], in0=phi_b_row[:, :], scalar=zsum[:, i:i + 1],
                                               in1=bank[bank_of(f"T{i}")][:, 0:CI],
                                               op0=ALU.mult, op1=ALU.add).then_inc(drained, 1)

            def split_t(b, n, i):
                dve.wait_ge(t_rounded, CB * b + n + 1)
                low(TL[:, i, :], T_full[:, i, :], TH[:, i, :]).then_inc(t_split, 1)

            def add_up(b, n, last):
                j, h = n // NH, n % NH
                dve.wait_ge(filled, done(b, f"out{n}", last))
                dve.wait_ge(slot_moved[n % SLOTS], 16 * (OUTS // SLOTS) * b + 16 * (n // SLOTS + 1))
                nc.vector.scalar_tensor_tensor(out=stage[:, n % SLOTS, :], in0=bank[bank_of(f"out{n}", last)][:, :],
                                               scalar=shift[:, j:j + 1], in1=X[:, j, h * BANK:(h + 1) * BANK],
                                               op0=ALU.add, op1=ALU.add).then_inc(drained, 1)

            def batch(b, last):
                for j in range(CB):
                    dve.wait_ge(z_summed, CB * b + j + 1)
                    if j == 0:
                        nc.vector.tensor_scalar(phi_sum_parts[:, :], phiT[:, 0, :], zsum[:, 0:1], None,
                                                ALU.mult).then_inc(parts_step, 1)
                        continue
                    dve.wait_ge(parts_step, CB * b + j)
                    nc.vector.scalar_tensor_tensor(out=phi_sum_parts[:, :], in0=phiT[:, j, :], scalar=zsum[:, j:j + 1],
                                                   in1=phi_sum_parts[:, :], op0=ALU.mult,
                                                   op1=ALU.add).then_inc(parts_step, 1)
                split_s(b, 0)
                split_x(b, 0)
                split_x(b, 1)
                split_s(b, 1)
                split_x(b, 2)
                split_x(b, 3)
                split_s(b, 2)
                split_s(b, 3)
                split_theta(b, 0)
                m0, m1 = (bank[bank_of(f"mirror{n}")] for n in range(2))
                dve.wait_ge(mirror_rounded, 2 * b + 1)
                low(SL[:, 1:4, 0:P], m0[:, 0:3 * P].rearrange("p (a c) -> p a c", c=P), SH[:, 1:4, 0:P]).then_inc(drained, 1)
                dve.wait_ge(mirror_rounded, 2 * b + 2)
                nc.vector.scalar_tensor_tensor(out=phi_sum[:, :], in0=cols[:, PHI_B:PHI_B + IB], scalar=float(N),
                                               in1=m1[:, 3 * P:3 * P + IB], op0=ALU.mult, op1=ALU.add).then_inc(phi_summed, 1)
                low(SL[:, 2:4, P:2 * P], m1[:, 0:2 * P].rearrange("p (a c) -> p a c", c=P), SH[:, 2:4, P:2 * P])
                low(SL[:, 3, 2 * P:3 * P], m1[:, 2 * P:3 * P], SH[:, 3, 2 * P:3 * P]).then_inc(drained, 1)
                split_theta(b, 1)
                whole_t(b, 3, last)
                whole_t(b, 2, last)
                split_t(b, 0, 3)
                whole_t(b, 1, last)
                split_t(b, 1, 2)
                whole_t(b, 0, last)
                split_t(b, 2, 1)
                split_t(b, 3, 0)
                dve.wait_ge(phi_summed, b + 1)
                for m in range(IB):
                    dve.wait_ge(filled, done(b, f"L{m}", last))
                    nc.vector.scalar_tensor_tensor(out=L_full[:, m, :], in0=h_row[:, :], scalar=phi_sum[:, m:m + 1],
                                                   in1=bank[bank_of(f"L{m}")][:, :],
                                                   op0=ALU.mult, op1=ALU.add).then_inc(drained, 1)
                for m in range(IB):
                    dve.wait_ge(l_rounded, IB * b + m + 1)
                    low(LL[:, m, :], L_full[:, m, :], LH[:, m, :]).then_inc(l_split, 1)
                split_theta(b, 2)
                split_theta(b, 3)
                for n in range(OUTS):
                    if not last:
                        split_zt(NB * b + NB + n + 1, n, bank[bank_of(f"next{n}")])
                    add_up(b, n, last)

            dve.wait_ge(params_loaded, 32)
            nc.vector.tensor_scalar(a_col[:, 0, :], cols[:, VAR:VAR + CB], EPS, None, ALU.add).then_inc(var_eps, 1)
            dve.wait_ge(rows_loaded, 16)
            nc.vector.tensor_scalar(var_row, var_row, EPS, None, ALU.add).then_inc(var_eps, 1)
            dve.wait_ge(ident_made, 1)
            for m in range(IB):
                nc.vector.tensor_scalar(gb_wide[:, m, :], ones[:, :], cols[:, G_B + m:G_B + m + 1], None,
                                        ALU.mult).then_inc(consts_made, 1)
            dve.wait_ge(rooted, 2)
            for v, root, r, gamma, a, by in (
                (var_row, newton_a, newton_b, gamma_row, A_row[:, :], 1.0 / N),
                (a_col[:, 0, :], a_col[:, 1, :], a_col[:, 2, :], cols[:, GAMMA:GAMMA + CB], a_col[:, 3, :], 1.0),
            ):
                link(nc.vector.reciprocal(r, root))
                link(nc.vector.tensor_tensor(root, r, r, ALU.mult))
                link(nc.vector.tensor_tensor(root, root, v, ALU.mult))
                link(nc.vector.tensor_scalar(root, root, -0.5, 1.5, ALU.mult, ALU.add))
                link(nc.vector.tensor_tensor(r, r, root, ALU.mult))
                link(nc.vector.scalar_tensor_tensor(out=a, in0=r, scalar=by, in1=gamma, op0=ALU.mult, op1=ALU.mult))
            for i in range(CB):
                dve.wait_ge(v_filled, i + 1)
                nc.vector.tensor_tensor(V_full[:, i, :], bank[i][:, :], A_row[:, :], ALU.mult).then_inc(v_scaled, 1)
            dve.wait_ge(v_filled, CB + 1)
            nc.vector.tensor_tensor(h_row[:, :], bank[CB][:, :], A_row[:, :], ALU.mult).then_inc(v_scaled, 1)
            link(nc.vector.tensor_tensor(shift[:, :], cols[:, W_B:W_B + CB], cols[:, MEAN:MEAN + CB], ALU.subtract))
            link(nc.vector.tensor_tensor(shift[:, :], shift[:, :], a_col[:, 3, :], ALU.mult))
            link(nc.vector.tensor_tensor(shift[:, :], shift[:, :], cols[:, BETA:BETA + CB], ALU.add))
            for n in range(NB):
                split_zt(n + 1, n, bank[n])
            dve.wait_ge(w_rounded, 1)
            low(thetaTL[:, :, :], thetaT_raw, thetaTH[:, :, :]).then_inc(w_split, 1)
            dve.wait_ge(w_rounded, 2)
            low(phiTL[:, :, :], phiT[:, :, :], phiTH[:, :, :]).then_inc(w_split, 1)
            dve.wait_ge(v_rounded, 1)
            low(VL[:, :, :], V_full[:, :, :], VH[:, :, :]).then_inc(v_split, 1)
            with dve.Fori(0, B - 1) as b:
                batch(b, False)
            batch(B - 1, True)

        @block.tensor
        def _(pe):
            def product(dst, blocks):
                for n, (stationary, moving) in enumerate(blocks):
                    for q, (s, m) in enumerate(PARTS):
                        last = nc.tensor.matmul(dst, stationary(s), moving(m), start=(n == 0 and q == 0),
                                                stop=(n == len(blocks) - 1 and q == len(PARTS) - 1))
                return last

            def transposes(n, bk):
                for j in range(CB):
                    last = nc.tensor.transpose(bk[:, j * P:(j + 1) * P], Z[:, j, n * P:(n + 1) * P], ident[:, :])
                last.then_inc(filled, 1)

            def gram(b, i, last):
                pe.wait_ge(drained, reusable(b, f"S{i}", last))
                bk = bank[bank_of(f"S{i}")]
                for n in range(NB):
                    if i == 0:
                        pe.wait_ge(drained, PER_BATCH * b + n + 1)
                    for q, (s, m) in enumerate(PARTS):
                        mm = nc.tensor.matmul(bk[:, i * P:C], ZT[s][:, n, i * P:(i + 1) * P], ZT[m][:, n, i * P:C],
                                              start=(n == 0 and q == 0), stop=(n == NB - 1 and q == 2))
                mm.then_inc(filled, 1)

            def theta(b, n, last):
                m, h = n % IB, n // IB
                pe.wait_ge(drained, reusable(b, f"theta{n}", last))
                product(bank[bank_of(f"theta{n}")][:, :],
                        [(lambda s, j=j: THETA_W[s][:, j, m * P:(m + 1) * P],
                          lambda q, j=j: XX[q][:, j, h * BANK:(h + 1) * BANK]) for j in range(CB)]).then_inc(filled, 1)

            def batch(b, last):
                for i in range(CB):
                    gram(b, i, last)
                pe.wait_ge(x_split, CB * b + CB)
                theta(b, 0, last)
                pe.wait_ge(drained, reusable(b, "mirror0", last))
                for q, j in enumerate((1, 2, 3)):
                    mm = nc.tensor.transpose(bank[bank_of("mirror0")][:, q * P:(q + 1) * P],
                                             full[:, 0, j * P:(j + 1) * P], ident[:, :])
                mm.then_inc(filled, 1)
                pe.wait_ge(drained, done(b, "S2", last))
                bk = bank[bank_of("mirror1")]
                for q, (i, j) in enumerate(((1, 2), (1, 3), (2, 3))):
                    nc.tensor.transpose(bk[:, q * P:(q + 1) * P], full[:, i, j * P:(j + 1) * P], ident[:, :])
                pe.wait_ge(parts_step, CB * b + CB)
                for m in range(IB):
                    mm = nc.tensor.matmul(bk[:, 3 * P + m:3 * P + m + 1], phi_sum_parts[:, m * P:(m + 1) * P],
                                          ones[:, 0:1], start=True, stop=True)
                mm.then_inc(filled, 1)
                theta(b, 1, last)
                pe.wait_ge(drained, done(b, "mirror1", last))
                for i in (3, 2, 1, 0):
                    product(bank[bank_of(f"T{i}")][:, 0:CI],
                            [(lambda s, j=j: SS[s][:, j, i * P:(i + 1) * P],
                              lambda q, j=j: PHI_W[q][:, j, :]) for j in range(CB)]).then_inc(filled, 1)
                pe.wait_ge(drained, reusable(b, "L1", last))
                for n, j in enumerate((3, 2, 1, 0)):
                    pe.wait_ge(t_split, CB * b + n + 1)
                    for m in range(IB):
                        for q, (s, v) in enumerate(PARTS):
                            mm = nc.tensor.matmul(bank[bank_of(f"L{m}")][:, :], TT[s][:, j, m * P:(m + 1) * P],
                                                  VV[v][:, j, :], start=(n == 0 and q == 0), stop=(n == CB - 1 and q == 2))
                        if n == CB - 1:
                            mm.then_inc(filled, 1)
                theta(b, 2, last)
                theta(b, 3, last)
                for n in range(OUTS):
                    if not last:
                        pe.wait_ge(drained, reusable(b, f"next{n}"))
                        if n == 0:
                            for j in range(CB):
                                pe.wait_ge(z_loaded[j], 16 * b + 32)
                        transposes(n, bank[bank_of(f"next{n}")])
                    pe.wait_ge(drained, reusable(b, f"out{n}", last))
                    if n == 0:
                        pe.wait_ge(l_split, IB * b + IB)
                    if n < 2:
                        pe.wait_ge(drained, done(b, f"theta{IB * n + IB - 1}", last))
                    j, h = n // NH, n % NH
                    product(bank[bank_of(f"out{n}", last)][:, :],
                            [(lambda s, m=m: LLT[s][:, m, j * P:(j + 1) * P],
                              lambda q, m=m: TH_[q][:, m, h * BANK:(h + 1) * BANK]) for m in range(IB)]).then_inc(filled, 1)

            for i in range(SLOTS):
                pe.wait_ge(slot_moved[i], 16)
            for i in range(CB):
                for m in range(IB):
                    mm = nc.tensor.matmul(bank[i][:, :], gw_raw[:, m, i * P:(i + 1) * P], wwT_raw[:, m, :],
                                          start=(m == 0), stop=(m == IB - 1))
                mm.then_inc(v_filled, 1)
            pe.wait_ge(consts_made, IB)
            for m in range(IB):
                mm = nc.tensor.matmul(bank[CB][:, :], gb_wide[:, m, :], wwT_raw[:, m, :],
                                      start=(m == 0), stop=(m == IB - 1))
            mm.then_inc(v_filled, 1)
            pe.wait_ge(ident_made, 2)
            for j in range(CB):
                pe.wait_ge(z_loaded[j], 16)
            for n in range(NB):
                if n <= CB:
                    pe.wait_ge(v_scaled, n + 1)
                transposes(n, bank[n])
            pe.wait_ge(w_split, 2)
            pe.wait_ge(v_split, 1)
            with pe.Fori(0, B - 1) as b:
                batch(b, False)
            batch(B - 1, True)


def kernel(**inputs):
    import numpy as np
    import concourse.bacc as bacc
    from concourse.bass_utils import run_bass_kernel_spmd

    def of(name):
        return np.ascontiguousarray(inputs[name])

    def blocks(name):
        return of(f"L0_xattn_{name}").reshape(-1, P).T

    x = of("x")
    columns = np.concatenate([blocks(n) for n in
                              ("theta_b", "phi_b", "g_b", "w_b", "bn_mean", "bn_beta", "bn_gamma", "bn_var")], axis=1)
    rows = np.concatenate([of(f"L0_xattn_{n}") for n in ("phi_b", "bn_gamma", "bn_var")])[None, :]
    arrays = {
        "x": x,
        "ctx": of("ctx_2048"),
        "theta_wT": np.ascontiguousarray(of("L0_xattn_theta_w").T),
        "phi_wT": np.ascontiguousarray(of("L0_xattn_phi_w").T),
        "g_w": of("L0_xattn_g_w"),
        "w_wT": np.ascontiguousarray(of("L0_xattn_w_w").T),
        "columns": np.ascontiguousarray(columns),
        "rows": np.ascontiguousarray(rows),
    }
    nc = bacc.Bacc("TRN2", target_bir_lowering=False, num_devices=1)
    args = [nc.dram_tensor(f"{name}_dram", a.shape, mybir.dt.from_np(a.dtype), kind="ExternalInput").ap()
            for name, a in arrays.items()]
    args.append(nc.dram_tensor("out_dram", x.shape, mybir.dt.from_np(x.dtype), kind="ExternalOutput").ap())
    xattn(nc, *args)
    r = run_bass_kernel_spmd(nc, [{f"{name}_dram": a for name, a in arrays.items()}], core_ids=[0])
    return r.results[0]["out_dram"]
```

```python
from contextlib import ExitStack

import concourse.bass as bass
from concourse import mybir

P = 128
BANKS = 8
BANK = 512


def xattn(nc, x, ctx_in, theta_wT, phi_wT, g_w, w_wT, columns, rows, out):
    f32 = mybir.dt.float32
    f32r = mybir.dt.float32r
    ALU = mybir.AluOpType
    ACT = mybir.ActivationFunctionType

    B, C, N = x.shape
    CI = theta_wT.shape[1]
    CB, IB, NB = C // P, CI // P, N // P
    NH = N // BANK
    Q = 32
    QUARTERS = P // Q
    NQ = N // QUARTERS
    EPS = 1e-5
    SLOTS = 4
    OUTS = CB * NH
    BW = P + 2

    THETA_B, PHI_B, G_B = 0, IB, 2 * IB
    W_B, MEAN, BETA, GAMMA, VAR = (3 * IB + n * CB for n in range(5))
    COLS = columns.shape[1]

    TASKS = (["S0", "S1", "S2", "S3", "theta0", "mirror0", "mirror1", "theta1"]
             + ["T0", "T1", "T2", "T3", "L0", "L1", "theta2", "theta3"] + [f"out{n}" for n in range(OUTS)])
    PER_BATCH = len(TASKS)

    def done(b, task):
        return PER_BATCH * b + BANKS + TASKS.index(task) + 1

    def half_of(n):
        return n // (2 * NH) * 2 + n % 2, n // 2 % NH

    def reusable(b, task):
        return done(b, task) - BANKS

    S_BLOCKS = [slice(0, 3), slice(1, 4), slice(2, 4), slice(0, 4, 3)]
    WHOLE = [(slice(1, 3), slice(1, 3)), (slice(2, 4), slice(1, 3)), (slice(3, 4), slice(1, 2)), (slice(0, 1), slice(0, 1))]
    MIRRORS = [[(0, 1), (0, 2), (1, 2)], [(1, 3), (2, 3), (3, 0)]]

    V_AFTER = (0, 3, 5, 7)

    with ExitStack() as ctx:
        def sb(name, shape, dt=f32):
            return ctx.enter_context(nc.sbuf_tensor(name, shape, dt))

        def sem(name):
            return ctx.enter_context(nc.semaphore(name))

        Z = sb("Z", [P, C // Q, NQ])
        X = sb("X", [P, CB, N])
        XH, XL = sb("XH", [P, CB, N], f32r), sb("XL", [P, CB, N], f32r)
        ZTH, ZTL = sb("ZTH", [P, NB, CB, BW], f32r), sb("ZTL", [P, NB, CB, BW], f32r)
        ring = sb("ring", [P, 2, C])
        full = sb("full", [P, CB, CB, P])
        SH, SL = sb("SH", [P, CB, CB, P], f32r), sb("SL", [P, CB, CB, P], f32r)
        thH, thL = sb("thH", [P, IB, N], f32r), sb("thL", [P, IB, N], f32r)
        TH, TL = sb("TH", [P, CB, CI], f32r), sb("TL", [P, CB, CI], f32r)
        LH, LL = sb("LH", [P, IB, C], f32r), sb("LL", [P, IB, C], f32r)
        stage = sb("stage", [P, SLOTS, BANK])
        phiT = sb("phiT", [P, CB, CI])
        phiTH, phiTL = sb("phiTH", [P, CB, CI], f32r), sb("phiTL", [P, CB, CI], f32r)
        thetaTH, thetaTL = sb("thetaTH", [P, CB, CI], f32r), sb("thetaTL", [P, CB, CI], f32r)
        VH, VL = sb("VH", [P, CB, C], f32r), sb("VL", [P, CB, C], f32r)
        cols = sb("cols", [P, COLS])
        phi_b_row = sb("phi_b_row", [P, CI])
        h_row = sb("h_row", [P, C])
        ident = sb("ident", [P, P])
        ones = sb("ones", [P, P])
        zsum = sb("zsum", [P, CB])
        phi_sum_parts = sb("phi_sum_parts", [P, CI])
        phi_sum = sb("phi_sum", [P, IB])
        shift = sb("shift", [P, CB])
        scale = sb("scale", [P, CB])
        newton = sb("newton", [P, 3, CB])

        full_rows = full[:, :, :, :].rearrange("p a b c -> p a (b c)")
        T_full = full_rows[:, 0:2, :].rearrange("p a (b i) -> p (a b) i", i=CI)
        L_full = full_rows[:, 2:4, :]
        gw_raw, wwT_raw = stage[:, 0:IB, :], stage[:, IB:2 * IB, :]
        h_parts = full_rows[:, 0:IB, :]
        thetaT_raw = full_rows[:, 2:4, :].rearrange("p a (b i) -> p (a b) i", i=CI)

        bank = [ctx.enter_context(nc.psum_tensor(f"bank{i}", [P, BANK], f32)) for i in range(BANKS)]

        def bank_of(task):
            return bank[TASKS.index(task) % BANKS]

        params_loaded, thetaT_loaded, phiT_loaded = sem("params_loaded"), sem("thetaT_loaded"), sem("phiT_loaded")
        slot_moved = [sem(f"slot_moved{i}") for i in range(SLOTS)]
        z_loaded = [sem(f"z_loaded{a}") for a in range(QUARTERS)]
        x_loaded = [sem(f"x_loaded{j}") for j in range(CB)]
        ident_zeroed, ident_made, ones_made = sem("ident_zeroed"), sem("ident_made"), sem("ones_made")
        var_ready, rooted, chained = sem("var_ready"), sem("rooted"), sem("chained")
        scales_made, h_parts_made = sem("scales_made"), sem("h_parts_made")
        z_half_loaded = [sem(f"z_half_loaded{a}") for a in range(QUARTERS)]
        scaled = sem("scaled")
        v_rounded, w_rounded = sem("v_rounded"), sem("w_rounded")
        theta_w_split, phi_w_split = sem("theta_w_split"), sem("phi_w_split")
        filled, drained = sem("filled"), sem("drained")
        zt_made, zt_rounded, zt_split = sem("zt_made"), sem("zt_rounded"), sem("zt_split")
        x_rounded, x_split = sem("x_rounded"), sem("x_split")
        s_rounded, mirror_rounded, theta_rounded = sem("s_rounded"), sem("mirror_rounded"), sem("theta_rounded")
        parts_step, phi_summed = sem("parts_step"), sem("phi_summed")
        t_rounded, t_split, l_rounded, l_split = sem("t_rounded"), sem("t_split"), sem("l_rounded"), sem("l_split")

        PARTS = ((0, 0), (0, 1), (1, 0))
        ZT, XX, SS, THETA, TT, LX = (ZTH, ZTL), (XH, XL), (SH, SL), (thH, thL), (TH, TL), (LH, LL)
        THETA_W, PHI_W, VV = (thetaTH, thetaTL), (phiTH, phiTL), (VH, VL)

        def ring_blocks(n):
            return ring[:, n % 2, :].rearrange("p (a c) -> p a c", c=P)

        def s_row(t, i):
            return t[:, i, S_BLOCKS[i], :]

        def s_bank(i):
            n = len(range(CB)[S_BLOCKS[i]])
            return bank_of(f"S{i}")[:, 0:n * BW].rearrange("p (a c) -> p a c", c=BW)

        def mirrored(t, n):
            bk = bank_of(f"mirror{n}")[:, 0:3 * P].rearrange("p (a c) -> p a c", c=P)
            if n == 0:
                return (t[:, 1:3, 0, :], bk[:, 0:2, :]), (t[:, 2, 1, :], bk[:, 2, :])
            return (t[:, 3, 1:3, :], bk[:, 0:2, :]), (t[:, 0, 3, :], bk[:, 2, :])

        block = ctx.enter_context(nc.Block())

        @block.sync
        def _(sp):
            def load_z(b):
                for a in range(QUARTERS):
                    sp.dma_start(Z[a * Q:(a + 1) * Q, :, :],
                                 ctx_in[b, :, a * NQ:(a + 1) * NQ].rearrange("(g q) n -> q g n", q=Q)
                                 ).then_inc(z_loaded[a], 16)

            def load_x(b, j):
                sp.dma_start(X[:, j, :], x[b, j * P:(j + 1) * P, :]).then_inc(x_loaded[j], 16)

            def store(b, n):
                j, h = half_of(n)
                sp.dma_start(out[b, j * P:(j + 1) * P, h * BANK:(h + 1) * BANK],
                             stage[:, n % SLOTS, :]).then_inc(slot_moved[n % SLOTS], 16)

            sp.dma_start(cols[:, :], columns).then_inc(params_loaded, 16)
            for m in range(IB):
                sp.dma_start(wwT_raw[:, m, :], w_wT[m * P:(m + 1) * P, :]).then_inc(slot_moved[IB + m], 16)
                sp.dma_start(gw_raw[:, m, :], g_w[m * P:(m + 1) * P, :]).then_inc(slot_moved[m], 16)
            for half, loaded in ((0, z_half_loaded), (1, z_loaded)):
                for a in range(QUARTERS):
                    at = half * NQ // 2
                    sp.dma_start(Z[a * Q:(a + 1) * Q, :, at:at + NQ // 2],
                                 ctx_in[0, :, a * NQ + at:a * NQ + at + NQ // 2].rearrange("(g q) n -> q g n", q=Q)
                                 ).then_inc(loaded[a], 16)
            for j in range(CB):
                load_x(0, j)
            sp.dma_start(thetaT_raw, theta_wT.rearrange("(a p) i -> p a i", p=P)).then_inc(thetaT_loaded, 16)
            sp.dma_start(phiT[:, :, :], phi_wT.rearrange("(a p) i -> p a i", p=P)).then_inc(phiT_loaded, 16)
            sp.dma_start(phi_b_row[:, :], rows.to_broadcast([P, CI])).then_inc(phiT_loaded, 16)

            with sp.Fori(0, B - 1) as b:
                sp.wait_ge(zt_made, NB * b + NB)
                load_z(b + 1)
                for n in range(OUTS):
                    sp.wait_ge(drained, done(b, f"out{n}"))
                    store(b, n)
                    j, h = half_of(n)
                    if h == NH - 1:
                        load_x(b + 1, j)
            for n in range(OUTS):
                sp.wait_ge(drained, done(B - 1, f"out{n}"))
                store(B - 1, n)
            for i in range(SLOTS):
                sp.wait_ge(slot_moved[i], 16 * (1 + B * OUTS // SLOTS))

        @block.gpsimd
        def _(pool):
            nc.gpsimd.memset(ident[:, :], 0.0).then_inc(ident_zeroed, 1)
            nc.gpsimd.memset(ones[:, :], 1.0).then_inc(ones_made, 1)
            pool.wait_ge(ident_zeroed, 1)
            nc.gpsimd.affine_select(out=ident[:, :], in_=ident[:, :], compare_op=ALU.not_equal, fill=1.0, base=0,
                                    pattern=[[-1, P]], channel_multiplier=1).then_inc(ident_made, 1)

        @block.scalar
        def _(act):
            def round_zt(b, n):
                act.wait_ge(zt_made, NB * b + n + 1)
                nc.scalar.copy(ZTH[:, n, :, 0:P], ring_blocks(n)).then_inc(zt_rounded, 1)

            def round_x(b, j):
                act.wait_ge(x_loaded[j], 16 * b + 16)
                nc.scalar.copy(XH[:, j, :], X[:, j, :]).then_inc(x_rounded, 1)

            def round_s(b, i):
                act.wait_ge(filled, done(b, f"S{i}"))
                blocks, at = WHOLE[i]
                nc.scalar.copy(zsum[:, i:i + 1], s_bank(i)[:, 0, P:P + 1])
                nc.scalar.copy(full[:, i, blocks, :], s_bank(i)[:, at, 0:P])
                nc.scalar.copy(s_row(SH, i), s_bank(i)[:, :, 0:P]).then_inc(s_rounded, 1)

            def round_theta(b, n):
                m, h = n % IB, n // IB
                act.wait_ge(filled, done(b, f"theta{n}"))
                nc.scalar.activation(thH[:, m, h * BANK:(h + 1) * BANK], bank_of(f"theta{n}")[:, :],
                                     ACT.Identity, bias=cols[:, THETA_B + m:THETA_B + m + 1]).then_inc(theta_rounded, 1)

            def round_mirror(b, n):
                act.wait_ge(filled, done(b, f"mirror{n}"))
                for place, made in mirrored(SH, n):
                    last = nc.scalar.copy(place, made)
                last.then_inc(mirror_rounded, 1)

            def round_t(b, i):
                act.wait_ge(drained, done(b, f"T{i}"))
                nc.scalar.copy(TH[:, i, :], T_full[:, i, :]).then_inc(t_rounded, 1)

            def round_l(b, m):
                act.wait_ge(drained, done(b, f"L{m}"))
                nc.scalar.copy(LH[:, m, :], L_full[:, m, :]).then_inc(l_rounded, 1)

            def scale_out(b, n):
                j, _ = half_of(n)
                act.wait_ge(filled, done(b, f"out{n}"))
                act.wait_ge(slot_moved[n % SLOTS], 16 * (OUTS // SLOTS) * b + 16 * (n // SLOTS + 1))
                nc.scalar.activation(stage[:, n % SLOTS, :], bank_of(f"out{n}")[:, :], ACT.Identity,
                                     bias=shift[:, j:j + 1], scale=scale[:, j:j + 1]).then_inc(scaled, 1)

            def batch(b, last):
                def round_next_zt(n):
                    if not last:
                        round_zt(b + 1, n)

                round_s(b, 0)
                round_x(b, 0)
                round_x(b, 1)
                round_s(b, 1)
                round_x(b, 2)
                round_x(b, 3)
                round_s(b, 2)
                round_s(b, 3)
                round_next_zt(0)
                round_next_zt(1)
                round_theta(b, 0)
                round_mirror(b, 0)
                round_mirror(b, 1)
                round_theta(b, 1)
                for i in range(CB):
                    round_t(b, i)
                    if i < CB - 1:
                        round_next_zt(2 + i)
                round_next_zt(5)
                round_next_zt(6)
                round_next_zt(7)
                round_l(b, 0)
                round_l(b, 1)
                round_theta(b, 2)
                round_theta(b, 3)
                for n in range(OUTS):
                    scale_out(b, n)

            act.wait_ge(var_ready, 1)
            nc.scalar.activation(newton[:, 1, :], newton[:, 0, :], ACT.Sqrt).then_inc(rooted, 1)
            for n in range(NB):
                round_zt(0, n)
                if n in V_AFTER:
                    i = V_AFTER.index(n)
                    act.wait_ge(filled, i + 1)
                    nc.scalar.copy(VH[:, i, :], bank[i][:, :]).then_inc(v_rounded, 1)
            act.wait_ge(thetaT_loaded, 16)
            nc.scalar.copy(thetaTH[:, :, :], thetaT_raw).then_inc(w_rounded, 1)
            act.wait_ge(phiT_loaded, 32)
            nc.scalar.copy(phiTH[:, :, :], phiT[:, :, :]).then_inc(w_rounded, 1)
            act.wait_ge(theta_w_split, 1)
            act.wait_ge(scales_made, 1)
            with act.Fori(0, B - 1) as b:
                batch(b, False)
            batch(B - 1, True)

        @block.vector
        def _(dve):
            links = [0]

            def link(instruction):
                links[0] += 1
                instruction.then_inc(chained, 1)
                dve.wait_ge(chained, links[0])

            def low(dst, whole, high):
                return nc.vector.tensor_tensor(dst, whole, high.bitcast(f32), ALU.subtract)

            def make_zt(b, n, first=False):
                if not first:
                    dve.wait_ge(zt_split, NB * b + n - 1)
                nc.vector.transpose(ring[:, n % 2, :].rearrange("p (g q) -> p g q", q=Q),
                                    Z[:, :, n * Q:(n + 1) * Q]).then_inc(zt_made, 1)

            def split_zt(b, n):
                dve.wait_ge(zt_rounded, NB * b + n + 1)
                low(ZTL[:, n, :, 0:P], ring_blocks(n), ZTH[:, n, :, 0:P]).then_inc(zt_split, 1)

            def split_x(b, j):
                dve.wait_ge(x_rounded, CB * b + j + 1)
                low(XL[:, j, :], X[:, j, :], XH[:, j, :]).then_inc(x_split, 1)

            def split_s(b, i):
                dve.wait_ge(s_rounded, CB * b + i + 1)
                low(s_row(SL, i), s_bank(i)[:, :, 0:P], s_row(SH, i)).then_inc(drained, 1)

            def sum_phi(b, j):
                if j == 0:
                    nc.vector.tensor_scalar(phi_sum_parts[:, :], phiT[:, 0, :], zsum[:, 0:1], None,
                                            ALU.mult).then_inc(parts_step, 1)
                    return
                dve.wait_ge(parts_step, CB * b + j)
                nc.vector.scalar_tensor_tensor(out=phi_sum_parts[:, :], in0=phiT[:, j, :], scalar=zsum[:, j:j + 1],
                                               in1=phi_sum_parts[:, :], op0=ALU.mult,
                                               op1=ALU.add).then_inc(parts_step, 1)

            def split_theta(b, n):
                m, h = n % IB, n // IB
                part = slice(h * BANK, (h + 1) * BANK)
                dve.wait_ge(theta_rounded, IB * NH * b + n + 1)
                nc.vector.scalar_tensor_tensor(out=thL[:, m, part], in0=bank_of(f"theta{n}")[:, :],
                                               scalar=cols[:, THETA_B + m:THETA_B + m + 1],
                                               in1=thH[:, m, part].bitcast(f32),
                                               op0=ALU.add, op1=ALU.subtract).then_inc(drained, 1)

            def split_mirror(b, n):
                dve.wait_ge(mirror_rounded, 2 * b + n + 1)
                for (place, made), (high, _) in zip(mirrored(SL, n), mirrored(SH, n)):
                    last = low(place, made, high)
                last.then_inc(drained, 1)

            def whole_t(b, i):
                dve.wait_ge(filled, done(b, f"T{i}"))
                if i == CB - 1:
                    nc.vector.scalar_tensor_tensor(out=phi_sum[:, :], in0=cols[:, PHI_B:PHI_B + IB], scalar=float(N),
                                                   in1=bank_of(f"T{i}")[:, CI:CI + IB],
                                                   op0=ALU.mult, op1=ALU.add).then_inc(phi_summed, 1)
                nc.vector.scalar_tensor_tensor(out=T_full[:, i, :], in0=phi_b_row[:, :], scalar=zsum[:, i:i + 1],
                                               in1=bank_of(f"T{i}")[:, 0:CI],
                                               op0=ALU.mult, op1=ALU.add).then_inc(drained, 1)

            def split_t(b, i):
                dve.wait_ge(t_rounded, CB * b + i + 1)
                low(TL[:, i, :], T_full[:, i, :], TH[:, i, :]).then_inc(t_split, 1)

            def whole_l(b, m):
                dve.wait_ge(filled, done(b, f"L{m}"))
                nc.vector.scalar_tensor_tensor(out=L_full[:, m, :], in0=h_row[:, :], scalar=phi_sum[:, m:m + 1],
                                               in1=bank_of(f"L{m}")[:, :],
                                               op0=ALU.mult, op1=ALU.add).then_inc(drained, 1)

            def split_l(b, m):
                dve.wait_ge(l_rounded, IB * b + m + 1)
                low(LL[:, m, :], L_full[:, m, :], LH[:, m, :]).then_inc(l_split, 1)

            def add_up(b, n):
                j, h = half_of(n)
                dve.wait_ge(scaled, OUTS * b + n + 1)
                nc.vector.tensor_tensor(stage[:, n % SLOTS, :], stage[:, n % SLOTS, :],
                                        X[:, j, h * BANK:(h + 1) * BANK], ALU.add).then_inc(drained, 1)

            def batch(b, last):
                def make_next_zt(n):
                    if last:
                        return
                    if n == 0:
                        for a in range(QUARTERS):
                            dve.wait_ge(z_loaded[a], 16 * b + 32)
                    make_zt(b + 1, n)

                def split_next_zt(n):
                    if not last:
                        split_zt(b + 1, n)

                split_s(b, 0)
                sum_phi(b, 0)
                split_x(b, 0)
                split_x(b, 1)
                split_s(b, 1)
                sum_phi(b, 1)
                split_x(b, 2)
                split_x(b, 3)
                split_s(b, 2)
                sum_phi(b, 2)
                split_s(b, 3)
                sum_phi(b, 3)
                make_next_zt(0)
                make_next_zt(1)
                split_theta(b, 0)
                split_mirror(b, 0)
                split_mirror(b, 1)
                split_next_zt(0)
                split_next_zt(1)
                split_theta(b, 1)
                whole_t(b, 0)
                make_next_zt(2)
                split_t(b, 0)
                whole_t(b, 1)
                make_next_zt(3)
                split_t(b, 1)
                whole_t(b, 2)
                split_next_zt(2)
                make_next_zt(4)
                split_t(b, 2)
                whole_t(b, 3)
                split_t(b, 3)
                for n in (5, 6, 7):
                    split_next_zt(n - 2)
                    make_next_zt(n)
                dve.wait_ge(phi_summed, b + 1)
                whole_l(b, 0)
                whole_l(b, 1)
                split_l(b, 0)
                split_l(b, 1)
                split_next_zt(6)
                split_next_zt(7)
                split_theta(b, 2)
                split_theta(b, 3)
                for n in range(OUTS):
                    add_up(b, n)

            def split_v(i):
                dve.wait_ge(v_rounded, i + 1)
                low(VL[:, i, :], bank[i][:, :], VH[:, i, :]).then_inc(drained, 1)

            dve.wait_ge(params_loaded, 16)
            v, root, r = (newton[:, n, :] for n in range(3))
            nc.vector.tensor_scalar(v, cols[:, VAR:VAR + CB], EPS, None, ALU.add).then_inc(var_ready, 1)
            for t, value in ((ZTH, 1.0), (ZTL, 0.0)):
                nc.vector.memset(t[:, :, :, P:BW].bitcast(f32), value)
            dve.wait_ge(rooted, 1)
            link(nc.vector.reciprocal(r, root))
            link(nc.vector.tensor_tensor(root, r, r, ALU.mult))
            link(nc.vector.tensor_tensor(root, root, v, ALU.mult))
            link(nc.vector.tensor_scalar(root, root, -0.5, 1.5, ALU.mult, ALU.add))
            link(nc.vector.tensor_tensor(r, r, root, ALU.mult))
            link(nc.vector.tensor_tensor(r, r, cols[:, GAMMA:GAMMA + CB], ALU.mult))
            link(nc.vector.tensor_tensor(shift[:, :], cols[:, W_B:W_B + CB], cols[:, MEAN:MEAN + CB], ALU.subtract))
            link(nc.vector.tensor_tensor(shift[:, :], shift[:, :], r, ALU.mult))
            link(nc.vector.tensor_tensor(shift[:, :], shift[:, :], cols[:, BETA:BETA + CB], ALU.add))
            nc.vector.tensor_scalar(scale[:, :], r, 1.0 / N, None, ALU.mult).then_inc(scales_made, 1)
            dve.wait_ge(slot_moved[IB], 16)
            link(nc.vector.tensor_scalar(h_parts[:, 0, :], wwT_raw[:, 0, :], cols[:, G_B:G_B + 1], None, ALU.mult))
            dve.wait_ge(slot_moved[IB + 1], 16)
            nc.vector.scalar_tensor_tensor(out=h_parts[:, 1, :], in0=wwT_raw[:, 1, :], scalar=cols[:, G_B + 1:G_B + 2],
                                           in1=h_parts[:, 0, :], op0=ALU.mult, op1=ALU.add).then_inc(h_parts_made, 1)
            for n in range(NB):
                for a in range(QUARTERS):
                    if n == 0:
                        dve.wait_ge(z_half_loaded[a], 16)
                    if n == NB // 2:
                        dve.wait_ge(z_loaded[a], 16)
                make_zt(0, n, first=n < 2)
                if n > 0:
                    split_zt(0, n - 1)
                if n == V_AFTER[0] + 1:
                    split_v(0)
            split_zt(0, NB - 1)
            for i in range(1, CB):
                split_v(i)
            dve.wait_ge(filled, BANKS)
            nc.vector.tensor_copy(h_row[:, :], bank[CB][:, :]).then_inc(drained, BANKS - CB)
            dve.wait_ge(w_rounded, 1)
            low(thetaTL[:, :, :], thetaT_raw, thetaTH[:, :, :]).then_inc(theta_w_split, 1)
            dve.wait_ge(w_rounded, 2)
            low(phiTL[:, :, :], phiT[:, :, :], phiTH[:, :, :]).then_inc(phi_w_split, 1)
            with dve.Fori(0, B - 1) as b:
                batch(b, False)
            batch(B - 1, True)

        @block.tensor
        def _(pe):
            def product(dst, blocks):
                for n, (stationary, moving) in enumerate(blocks):
                    for q, (s, m) in enumerate(PARTS):
                        last = nc.tensor.matmul(dst, stationary(s), moving(m), start=(n == 0 and q == 0),
                                                stop=(n == len(blocks) - 1 and q == len(PARTS) - 1))
                return last

            def gram(b, i):
                pe.wait_ge(drained, reusable(b, f"S{i}"))
                for n in range(NB):
                    if i == 0:
                        pe.wait_ge(zt_split, NB * b + n + 1)
                    for q, (s, m) in enumerate(PARTS):
                        mm = nc.tensor.matmul(s_bank(i), ZT[s][:, n, i, 0:P], ZT[m][:, n, S_BLOCKS[i], :],
                                              start=(n == 0 and q == 0), stop=(n == NB - 1 and q == 2))
                mm.then_inc(filled, 1)

            def theta(b, n):
                m, h = n % IB, n // IB
                pe.wait_ge(drained, reusable(b, f"theta{n}"))
                product(bank_of(f"theta{n}")[:, :],
                        [(lambda s, j=j: THETA_W[s][:, j, m * P:(m + 1) * P],
                          lambda q, j=j: XX[q][:, j, h * BANK:(h + 1) * BANK]) for j in range(CB)]).then_inc(filled, 1)

            def mirror(b, n):
                pe.wait_ge(drained, reusable(b, f"mirror{n}"))
                pe.wait_ge(drained, done(b, f"S{MIRRORS[n][-1][0]}"))
                for q, (i, j) in enumerate(MIRRORS[n]):
                    mm = nc.tensor.transpose(bank_of(f"mirror{n}")[:, q * P:(q + 1) * P],
                                             full[:, i, j, :], ident[:, :])
                mm.then_inc(filled, 1)

            def batch(b):
                for i in range(CB):
                    gram(b, i)
                pe.wait_ge(theta_w_split, 1)
                pe.wait_ge(x_split, CB * b + CB)
                theta(b, 0)
                mirror(b, 0)
                mirror(b, 1)
                theta(b, 1)
                pe.wait_ge(phi_w_split, 1)
                for i in range(CB):
                    if i < 2:
                        pe.wait_ge(drained, done(b, f"mirror{i}"))
                    mm = product(bank_of(f"T{i}")[:, 0:CI],
                                 [(lambda s, j=j: SS[s][:, j, i, :],
                                   lambda q, j=j: PHI_W[q][:, j, :]) for j in range(CB)])
                    if i == CB - 1:
                        pe.wait_ge(parts_step, CB * b + CB)
                        for m in range(IB):
                            mm = nc.tensor.matmul(bank_of(f"T{i}")[:, CI + m:CI + m + 1],
                                                  phi_sum_parts[:, m * P:(m + 1) * P], ones[:, 0:1],
                                                  start=True, stop=True)
                    mm.then_inc(filled, 1)
                pe.wait_ge(drained, reusable(b, "L1"))
                for j in range(CB):
                    pe.wait_ge(t_split, CB * b + j + 1)
                    for m in range(IB):
                        for q, (s, v) in enumerate(PARTS):
                            mm = nc.tensor.matmul(bank_of(f"L{m}")[:, :], TT[s][:, j, m * P:(m + 1) * P],
                                                  VV[v][:, j, :], start=(j == 0 and q == 0), stop=(j == CB - 1 and q == 2))
                        if j == CB - 1:
                            mm.then_inc(filled, 1)
                theta(b, 2)
                theta(b, 3)
                for n in range(OUTS):
                    pe.wait_ge(drained, reusable(b, f"out{n}"))
                    if n == 0:
                        pe.wait_ge(l_split, IB * b + IB)
                    if n == 2:
                        pe.wait_ge(drained, done(b, "theta3"))
                    j, h = half_of(n)
                    product(bank_of(f"out{n}")[:, :],
                            [(lambda s, m=m: LX[s][:, m, j * P:(j + 1) * P],
                              lambda q, m=m: THETA[q][:, m, h * BANK:(h + 1) * BANK]) for m in range(IB)]).then_inc(filled, 1)

            for i in range(CB):
                for m in range(IB):
                    if i == 0:
                        pe.wait_ge(slot_moved[m], 16)
                        pe.wait_ge(slot_moved[IB + m], 16)
                    mm = nc.tensor.matmul(bank[i][:, :], gw_raw[:, m, i * P:(i + 1) * P], wwT_raw[:, m, :],
                                          start=(m == 0), stop=(m == IB - 1))
                mm.then_inc(filled, 1)
            pe.wait_ge(ones_made, 1)
            pe.wait_ge(h_parts_made, 1)
            nc.tensor.matmul(bank[CB][:, :], ones[:, :], h_parts[:, 1, :], start=True, stop=True
                             ).then_inc(filled, BANKS - CB)
            pe.wait_ge(ident_made, 1)
            with pe.Fori(0, B - 1) as b:
                batch(b)
            batch(B - 1)


def kernel(**inputs):
    import numpy as np
    import concourse.bacc as bacc
    from concourse.bass_utils import run_bass_kernel_spmd

    def of(name):
        return np.ascontiguousarray(inputs[name])

    def blocks(name):
        return of(f"L0_xattn_{name}").reshape(-1, P).T

    x = of("x")
    columns = np.concatenate([blocks(n) for n in
                              ("theta_b", "phi_b", "g_b", "w_b", "bn_mean", "bn_beta", "bn_gamma", "bn_var")], axis=1)
    rows = of("L0_xattn_phi_b")[None, :]
    arrays = {
        "x": x,
        "ctx": of("ctx_2048"),
        "theta_wT": np.ascontiguousarray(of("L0_xattn_theta_w").T),
        "phi_wT": np.ascontiguousarray(of("L0_xattn_phi_w").T),
        "g_w": of("L0_xattn_g_w"),
        "w_wT": np.ascontiguousarray(of("L0_xattn_w_w").T),
        "columns": np.ascontiguousarray(columns),
        "rows": np.ascontiguousarray(rows),
    }
    nc = bacc.Bacc("TRN2", target_bir_lowering=False, num_devices=1)
    args = [nc.dram_tensor(f"{name}_dram", a.shape, mybir.dt.from_np(a.dtype), kind="ExternalInput").ap()
            for name, a in arrays.items()]
    args.append(nc.dram_tensor("out_dram", x.shape, mybir.dt.from_np(x.dtype), kind="ExternalOutput").ap())
    xattn(nc, *args)
    r = run_bass_kernel_spmd(nc, [{f"{name}_dram": a for name, a in arrays.items()}], core_ids=[0])
    return r.results[0]["out_dram"]
```

```python
from contextlib import ExitStack

import concourse.bass as bass
from concourse import mybir

P = 128
BANKS = 8
BANK = 512


def xattn(nc, x, ctx_in, theta_wT, phi_wT, g_w, w_wT, columns, rows, out):
    f32 = mybir.dt.float32
    f32r = mybir.dt.float32r
    ALU = mybir.AluOpType
    ACT = mybir.ActivationFunctionType

    B, C, N = x.shape
    CI = theta_wT.shape[1]
    CB, IB, NB = C // P, CI // P, N // P
    NH = N // BANK
    Q = 32
    QUARTERS = P // Q
    NQ = N // QUARTERS
    EPS = 1e-5
    SLOTS = 4
    OUTS = CB * NH
    FOLD_STEPS = 2 * QUARTERS + 1
    BW = P + 2
    RING = 3
    V_BANK = BANKS - CB
    WARM_UP = 8

    THETA_B, PHI_B, G_B = 0, IB, 2 * IB
    W_B, MEAN, BETA, GAMMA, VAR = (3 * IB + n * CB for n in range(5))
    COLS = columns.shape[1]

    TASKS = (["S0", "S1", "S2", "S3", "theta0", "mirror0", "mirror1", "theta1"]
             + ["T0", "T1", "T2", "T3", "L0", "L1", "theta2", "theta3"] + [f"out{n}" for n in range(OUTS)])
    PER_BATCH = len(TASKS)

    def done(b, task):
        return PER_BATCH * b + BANKS + TASKS.index(task) + 1

    def half_of(n):
        return n // (2 * NH) * 2 + n % 2, n // 2 % NH

    def reusable(b, task):
        return done(b, task) - BANKS

    S_BLOCKS = [slice(0, 3), slice(1, 4), slice(2, 4), slice(0, 4, 3)]
    WHOLE = [(slice(1, 3), slice(1, 3)), (slice(2, 4), slice(1, 3)), (slice(3, 4), slice(1, 2)), (slice(0, 1), slice(0, 1))]
    MIRRORS = [[(0, 1), (0, 2), (1, 2)], [(1, 3), (2, 3), (3, 0)]]

    with ExitStack() as ctx:
        def sb(name, shape, dt=f32):
            return ctx.enter_context(nc.sbuf_tensor(name, shape, dt))

        def sem(name):
            return ctx.enter_context(nc.semaphore(name))

        Z = sb("Z", [P, C // Q, NQ])
        X = sb("X", [P, CB, N])
        XH, XL = sb("XH", [P, CB, N], f32r), sb("XL", [P, CB, N], f32r)
        ZTH, ZTL = sb("ZTH", [P, NB, CB, BW], f32r), sb("ZTL", [P, NB, CB, BW], f32r)
        ring = sb("ring", [P, RING, C])
        full = sb("full", [P, CB, CB, P])
        SH, SL = sb("SH", [P, CB, CB, P], f32r), sb("SL", [P, CB, CB, P], f32r)
        thH, thL = sb("thH", [P, IB, N], f32r), sb("thL", [P, IB, N], f32r)
        TH, TL = sb("TH", [P, CB, CI], f32r), sb("TL", [P, CB, CI], f32r)
        LH, LL = sb("LH", [P, IB, C], f32r), sb("LL", [P, IB, C], f32r)
        stage = sb("stage", [P, SLOTS, BANK])
        phiT = sb("phiT", [P, CB, CI])
        phiTH, phiTL = sb("phiTH", [P, CB, CI], f32r), sb("phiTL", [P, CB, CI], f32r)
        thetaTH, thetaTL = sb("thetaTH", [P, CB, CI], f32r), sb("thetaTL", [P, CB, CI], f32r)
        VH, VL = sb("VH", [P, CB, C], f32r), sb("VL", [P, CB, C], f32r)
        cols = sb("cols", [P, COLS])
        phi_b_row = sb("phi_b_row", [P, CI])
        h_row = sb("h_row", [P, C])
        ident = sb("ident", [P, P])
        ones = sb("ones", [P, P])
        zsum = sb("zsum", [P, CB])
        phi_sum_parts = sb("phi_sum_parts", [P, CI])
        quarter_sums = sb("quarter_sums", [P, CI // Q])
        phi_b_folded = sb("phi_b_folded", [Q, CI // Q])
        phi_sum = sb("phi_sum", [P, IB])
        shift = sb("shift", [P, CB])
        scale = sb("scale", [P, CB])

        full_rows = full[:, :, :, :].rearrange("p a b c -> p a (b c)")
        T_full = full_rows[:, 0:2, :].rearrange("p a (b i) -> p (a b) i", i=CI)
        L_full = full_rows[:, 2:4, :]
        phi_sum_turned = full_rows[:, CB - 1, P:P + CI]
        folded = phi_sum_parts[0:Q, 0:QUARTERS * CI // Q].rearrange("q (a g) -> q a g", a=QUARTERS)
        newton = phi_sum_parts[:, 0:3 * CB].rearrange("p (n j) -> p n j", j=CB)
        gw_raw, wwT_raw = stage[:, 0:IB, :], stage[:, IB:2 * IB, :]
        h_parts = full_rows[:, 0:IB, :]
        thetaT_raw = full_rows[:, 2:4, :].rearrange("p a (b i) -> p (a b) i", i=CI)

        bank = [ctx.enter_context(nc.psum_tensor(f"bank{i}", [P, BANK], f32)) for i in range(BANKS)]

        def bank_of(task):
            return bank[TASKS.index(task) % BANKS]

        params_loaded, thetaT_loaded, phiT_loaded = sem("params_loaded"), sem("thetaT_loaded"), sem("phiT_loaded")
        slot_moved = [sem(f"slot_moved{i}") for i in range(SLOTS)]
        z_loaded = [sem(f"z_loaded{a}") for a in range(QUARTERS)]
        x_loaded = [sem(f"x_loaded{j}") for j in range(CB)]
        ident_zeroed, ident_made, ones_made = sem("ident_zeroed"), sem("ident_made"), sem("ones_made")
        var_ready, rooted, chained = sem("var_ready"), sem("rooted"), sem("chained")
        scales_made, h_parts_step = sem("scales_made"), sem("h_parts_step")
        z_half_loaded = [sem(f"z_half_loaded{a}") for a in range(QUARTERS)]
        scaled = sem("scaled")
        v_rounded, w_rounded = sem("v_rounded"), sem("w_rounded")
        theta_w_split, phi_w_split = sem("theta_w_split"), sem("phi_w_split")
        filled, drained = sem("filled"), sem("drained")
        zt_made, zt_rounded, zt_split = sem("zt_made"), sem("zt_rounded"), sem("zt_split")
        x_rounded, x_split = sem("x_rounded"), sem("x_split")
        s_rounded, mirror_rounded, theta_rounded = sem("s_rounded"), sem("mirror_rounded"), sem("theta_rounded")
        parts_step, turned, quarters_summed = sem("parts_step"), sem("turned"), sem("quarters_summed")
        fold_step = sem("fold_step")
        t_rounded, t_split, l_rounded, l_split = sem("t_rounded"), sem("t_split"), sem("l_rounded"), sem("l_split")

        PARTS = ((0, 0), (0, 1), (1, 0))
        ZT, XX, SS, THETA, TT, LX = (ZTH, ZTL), (XH, XL), (SH, SL), (thH, thL), (TH, TL), (LH, LL)
        THETA_W, PHI_W, VV = (thetaTH, thetaTL), (phiTH, phiTL), (VH, VL)

        def ring_blocks(n):
            return ring[:, n % RING, :].rearrange("p (a c) -> p a c", c=P)

        def s_row(t, i):
            return t[:, i, S_BLOCKS[i], :]

        def s_bank(i):
            n = len(range(CB)[S_BLOCKS[i]])
            return bank_of(f"S{i}")[:, 0:n * BW].rearrange("p (a c) -> p a c", c=BW)

        def mirrored(t, n):
            bk = bank_of(f"mirror{n}")[:, 0:3 * P].rearrange("p (a c) -> p a c", c=P)
            if n == 0:
                return (t[:, 1:3, 0, :], bk[:, 0:2, :]), (t[:, 2, 1, :], bk[:, 2, :])
            return (t[:, 3, 1:3, :], bk[:, 0:2, :]), (t[:, 0, 3, :], bk[:, 2, :])

        block = ctx.enter_context(nc.Block())

        @block.sync
        def _(sp):
            def load_z(b):
                for a in range(QUARTERS):
                    sp.dma_start(Z[a * Q:(a + 1) * Q, :, :],
                                 ctx_in[b, :, a * NQ:(a + 1) * NQ].rearrange("(g q) n -> q g n", q=Q)
                                 ).then_inc(z_loaded[a], 16)

            def load_x(b, j):
                sp.dma_start(X[:, j, :], x[b, j * P:(j + 1) * P, :]).then_inc(x_loaded[j], 16)

            def store(b, n):
                j, h = half_of(n)
                sp.dma_start(out[b, j * P:(j + 1) * P, h * BANK:(h + 1) * BANK],
                             stage[:, n % SLOTS, :]).then_inc(slot_moved[n % SLOTS], 16)

            def load_weights_of_v(m):
                sp.dma_start(gw_raw[:, m, :], g_w[m * P:(m + 1) * P, :]).then_inc(slot_moved[m], 16)
                sp.dma_start(wwT_raw[:, m, :], w_wT[m * P:(m + 1) * P, :]).then_inc(slot_moved[IB + m], 16)

            def load_first_z(half, loaded):
                for a in range(QUARTERS):
                    at = half * NQ // 2
                    sp.dma_start(Z[a * Q:(a + 1) * Q, :, at:at + NQ // 2],
                                 ctx_in[0, :, a * NQ + at:a * NQ + at + NQ // 2].rearrange("(g q) n -> q g n", q=Q)
                                 ).then_inc(loaded[a], 16)

            load_weights_of_v(0)
            sp.dma_start(cols[:, :], columns).then_inc(params_loaded, 16)
            load_first_z(0, z_half_loaded)
            load_weights_of_v(1)
            load_first_z(1, z_loaded)
            sp.dma_start(thetaT_raw, theta_wT.rearrange("(a p) i -> p a i", p=P)).then_inc(thetaT_loaded, 16)
            load_x(0, 0)
            load_x(0, 1)
            sp.dma_start(phiT[:, :, :], phi_wT.rearrange("(a p) i -> p a i", p=P)).then_inc(phiT_loaded, 16)
            sp.dma_start(phi_b_row[:, :], rows.to_broadcast([P, CI])).then_inc(phiT_loaded, 16)
            load_x(0, 2)
            load_x(0, 3)

            with sp.Fori(0, B - 1) as b:
                sp.wait_ge(zt_made, NB * b + NB)
                load_z(b + 1)
                for n in range(OUTS):
                    sp.wait_ge(drained, done(b, f"out{n}"))
                    store(b, n)
                    j, h = half_of(n)
                    if h == NH - 1:
                        load_x(b + 1, j)
            for n in range(OUTS):
                sp.wait_ge(drained, done(B - 1, f"out{n}"))
                store(B - 1, n)
            for i in range(SLOTS):
                sp.wait_ge(slot_moved[i], 16 * (1 + B * OUTS // SLOTS))

        @block.gpsimd
        def _(pool):
            nc.gpsimd.memset(ident[:, :], 0.0).then_inc(ident_zeroed, 1)
            nc.gpsimd.memset(ones[:, :], 1.0).then_inc(ones_made, 1)
            pool.wait_ge(ident_zeroed, 1)
            nc.gpsimd.affine_select(out=ident[:, :], in_=ident[:, :], compare_op=ALU.not_equal, fill=1.0, base=0,
                                    pattern=[[-1, P]], channel_multiplier=1).then_inc(ident_made, 1)
            pool.wait_ge(params_loaded, 16)
            for m in range(IB):
                pool.wait_ge(slot_moved[IB + m], 16)
                nc.gpsimd.tensor_scalar(h_parts[:, m, :], wwT_raw[:, m, :], cols[:, G_B + m:G_B + m + 1], None,
                                        ALU.mult).then_inc(h_parts_step, 1)
            pool.wait_ge(h_parts_step, IB)
            nc.gpsimd.tensor_tensor(h_parts[:, 0, :], h_parts[:, 0, :], h_parts[:, 1, :],
                                    ALU.add).then_inc(h_parts_step, 1)
            for n, (lowest, raw, high, split) in enumerate(((thetaTL, thetaT_raw, thetaTH, theta_w_split),
                                                            (phiTL, phiT, phiTH, phi_w_split))):
                pool.wait_ge(w_rounded, n + 1)
                nc.gpsimd.tensor_tensor(lowest[:, :, :], raw[:, :, :], high[:, :, :].bitcast(f32),
                                        ALU.subtract).then_inc(split, 1)
            by_block = phi_b_folded[:, :].rearrange("q (m s) -> q m s", s=QUARTERS)
            pool.wait_ge(phi_w_split, 1)
            for s in range(QUARTERS):
                if s > 0:
                    pool.wait_ge(fold_step, s)
                nc.gpsimd.tensor_scalar(by_block[:, :, s], cols[s * Q:(s + 1) * Q, PHI_B:PHI_B + IB], float(N), None,
                                        ALU.mult).then_inc(fold_step, 1)

            def fold(b):
                pool.wait_ge(quarters_summed, b + 1)
                for a in range(QUARTERS):
                    pool.wait_ge(fold_step, FOLD_STEPS * b + QUARTERS + a)
                    if a == 0:
                        nc.gpsimd.tensor_tensor(folded[:, a, :], quarter_sums[0:Q, :], phi_b_folded[:, :],
                                                ALU.add).then_inc(fold_step, 1)
                    else:
                        nc.gpsimd.tensor_tensor(folded[:, a, :], quarter_sums[a * Q:(a + 1) * Q, :],
                                                ones[a * Q:(a + 1) * Q, 0:CI // Q], ALU.mult).then_inc(fold_step, 1)
                pool.wait_ge(fold_step, FOLD_STEPS * b + 2 * QUARTERS)
                nc.gpsimd.tensor_tensor(folded[:, 0:2, :], folded[:, 0:2, :], folded[:, 2:4, :],
                                        ALU.add).then_inc(fold_step, 1)
                pair = folded[:, 0:2, :].rearrange("q a (m s) -> q a m s", s=QUARTERS)
                for s in range(QUARTERS):
                    pool.wait_ge(fold_step, FOLD_STEPS * b + 2 * QUARTERS + 1 + s)
                    nc.gpsimd.tensor_tensor(phi_sum[s * Q:(s + 1) * Q, :], pair[:, 0, :, s], pair[:, 1, :, s],
                                            ALU.add).then_inc(fold_step, 1)

            with pool.Fori(0, B) as b:
                fold(b)

        @block.scalar
        def _(act):
            def round_zt(b, n):
                act.wait_ge(zt_made, NB * b + n + 1)
                nc.scalar.copy(ZTH[:, n, :, 0:P], ring_blocks(n)).then_inc(zt_rounded, 1)

            def round_x(b, j):
                act.wait_ge(x_loaded[j], 16 * b + 16)
                nc.scalar.copy(XH[:, j, :], X[:, j, :]).then_inc(x_rounded, 1)

            def round_s(b, i):
                act.wait_ge(filled, done(b, f"S{i}"))
                blocks, at = WHOLE[i]
                nc.scalar.copy(zsum[:, i:i + 1], s_bank(i)[:, 0, P:P + 1])
                nc.scalar.copy(full[:, i, blocks, :], s_bank(i)[:, at, 0:P])
                nc.scalar.copy(s_row(SH, i), s_bank(i)[:, :, 0:P]).then_inc(s_rounded, 1)

            def round_theta(b, n):
                m, h = n % IB, n // IB
                act.wait_ge(filled, done(b, f"theta{n}"))
                nc.scalar.activation(thH[:, m, h * BANK:(h + 1) * BANK], bank_of(f"theta{n}")[:, :],
                                     ACT.Identity, bias=cols[:, THETA_B + m:THETA_B + m + 1]).then_inc(theta_rounded, 1)

            def round_mirror(b, n):
                act.wait_ge(filled, done(b, f"mirror{n}"))
                for place, made in mirrored(SH, n):
                    last = nc.scalar.copy(place, made)
                last.then_inc(mirror_rounded, 1)

            def round_t(b, i):
                act.wait_ge(drained, done(b, f"T{i}"))
                nc.scalar.copy(TH[:, i, :], T_full[:, i, :]).then_inc(t_rounded, 1)

            def round_l(b, m):
                act.wait_ge(drained, done(b, f"L{m}"))
                nc.scalar.copy(LH[:, m, :], L_full[:, m, :]).then_inc(l_rounded, 1)

            def scale_out(b, n):
                j, _ = half_of(n)
                act.wait_ge(filled, done(b, f"out{n}"))
                act.wait_ge(slot_moved[n % SLOTS], 16 * (OUTS // SLOTS) * b + 16 * (n // SLOTS + 1))
                nc.scalar.activation(stage[:, n % SLOTS, :], bank_of(f"out{n}")[:, :], ACT.Identity,
                                     bias=shift[:, j:j + 1], scale=scale[:, j:j + 1]).then_inc(scaled, 1)

            def batch(b, last):
                def round_next_zt(n):
                    if not last:
                        round_zt(b + 1, n)

                round_s(b, 0)
                round_x(b, 0)
                round_x(b, 1)
                round_s(b, 1)
                round_x(b, 2)
                round_x(b, 3)
                round_s(b, 2)
                round_s(b, 3)
                round_next_zt(0)
                round_next_zt(1)
                round_theta(b, 0)
                round_mirror(b, 0)
                round_mirror(b, 1)
                round_theta(b, 1)
                for i in range(CB):
                    round_t(b, i)
                    if i < CB - 1:
                        round_next_zt(2 + i)
                round_next_zt(5)
                round_next_zt(6)
                round_next_zt(7)
                round_l(b, 0)
                round_l(b, 1)
                round_theta(b, 2)
                round_theta(b, 3)
                for n in range(OUTS):
                    scale_out(b, n)

            act.wait_ge(var_ready, 1)
            nc.scalar.activation(newton[:, 1, :], newton[:, 0, :], ACT.Sqrt).then_inc(rooted, 1)
            for n in range(NB):
                round_zt(0, n)
            act.wait_ge(filled, BANKS)
            nc.scalar.copy(h_row[:, :], bank[V_BANK - 1][:, :]).then_inc(drained, 1)
            act.wait_ge(thetaT_loaded, 16)
            nc.scalar.copy(thetaTH[:, :, :], thetaT_raw).then_inc(w_rounded, 1)
            act.wait_ge(phiT_loaded, 32)
            nc.scalar.copy(phiTH[:, :, :], phiT[:, :, :]).then_inc(w_rounded, 1)
            for i in range(CB):
                nc.scalar.copy(VH[:, i, :], bank[V_BANK + i][:, :]).then_inc(v_rounded, 1)
            act.wait_ge(theta_w_split, 1)
            act.wait_ge(scales_made, 1)
            with act.Fori(0, B - 1) as b:
                batch(b, False)
            batch(B - 1, True)

        @block.vector
        def _(dve):
            links = [0]

            def link(instruction):
                links[0] += 1
                instruction.then_inc(chained, 1)
                dve.wait_ge(chained, links[0])

            def low(dst, whole, high):
                return nc.vector.tensor_tensor(dst, whole, high.bitcast(f32), ALU.subtract)

            def make_zt(b, n, first=False):
                if not first:
                    dve.wait_ge(zt_split, NB * b + n - RING + 1)
                nc.vector.transpose(ring[:, n % RING, :].rearrange("p (g q) -> p g q", q=Q),
                                    Z[:, :, n * Q:(n + 1) * Q]).then_inc(zt_made, 1)

            def split_zt(b, n):
                dve.wait_ge(zt_rounded, NB * b + n + 1)
                low(ZTL[:, n, :, 0:P], ring_blocks(n), ZTH[:, n, :, 0:P]).then_inc(zt_split, 1)

            def split_x(b, j):
                dve.wait_ge(x_rounded, CB * b + j + 1)
                low(XL[:, j, :], X[:, j, :], XH[:, j, :]).then_inc(x_split, 1)

            def split_s(b, i):
                dve.wait_ge(s_rounded, CB * b + i + 1)
                low(s_row(SL, i), s_bank(i)[:, :, 0:P], s_row(SH, i)).then_inc(drained, 1)

            def sum_phi(b, j):
                if j == 0:
                    nc.vector.tensor_scalar(phi_sum_parts[:, :], phiT[:, 0, :], zsum[:, 0:1], None,
                                            ALU.mult).then_inc(parts_step, 1)
                    return
                dve.wait_ge(parts_step, CB * b + j)
                nc.vector.scalar_tensor_tensor(out=phi_sum_parts[:, :], in0=phiT[:, j, :], scalar=zsum[:, j:j + 1],
                                               in1=phi_sum_parts[:, :], op0=ALU.mult,
                                               op1=ALU.add).then_inc(parts_step, 1)

            def turn_phi_sum(b):
                dve.wait_ge(parts_step, CB * b + CB)
                nc.vector.transpose(phi_sum_turned, phi_sum_parts[:, :]).then_inc(turned, 1)

            def sum_quarters(b):
                dve.wait_ge(turned, b + 1)
                nc.vector.tensor_reduce(quarter_sums[:, :], phi_sum_turned.rearrange("p (g q) -> p g q", q=Q),
                                        mybir.AxisListType.X, ALU.add).then_inc(quarters_summed, 1)

            def split_theta(b, n):
                m, h = n % IB, n // IB
                part = slice(h * BANK, (h + 1) * BANK)
                dve.wait_ge(theta_rounded, IB * NH * b + n + 1)
                nc.vector.scalar_tensor_tensor(out=thL[:, m, part], in0=bank_of(f"theta{n}")[:, :],
                                               scalar=cols[:, THETA_B + m:THETA_B + m + 1],
                                               in1=thH[:, m, part].bitcast(f32),
                                               op0=ALU.add, op1=ALU.subtract).then_inc(drained, 1)

            def split_mirror(b, n):
                dve.wait_ge(mirror_rounded, 2 * b + n + 1)
                for (place, made), (high, _) in zip(mirrored(SL, n), mirrored(SH, n)):
                    last = low(place, made, high)
                last.then_inc(drained, 1)

            def whole_t(b, i):
                dve.wait_ge(filled, done(b, f"T{i}"))
                nc.vector.scalar_tensor_tensor(out=T_full[:, i, :], in0=phi_b_row[:, :], scalar=zsum[:, i:i + 1],
                                               in1=bank_of(f"T{i}")[:, 0:CI],
                                               op0=ALU.mult, op1=ALU.add).then_inc(drained, 1)

            def split_t(b, i):
                dve.wait_ge(t_rounded, CB * b + i + 1)
                low(TL[:, i, :], T_full[:, i, :], TH[:, i, :]).then_inc(t_split, 1)

            def whole_l(b, m):
                dve.wait_ge(filled, done(b, f"L{m}"))
                nc.vector.scalar_tensor_tensor(out=L_full[:, m, :], in0=h_row[:, :], scalar=phi_sum[:, m:m + 1],
                                               in1=bank_of(f"L{m}")[:, :],
                                               op0=ALU.mult, op1=ALU.add).then_inc(drained, 1)

            def split_l(b, m):
                dve.wait_ge(l_rounded, IB * b + m + 1)
                low(LL[:, m, :], L_full[:, m, :], LH[:, m, :]).then_inc(l_split, 1)

            def add_up(b, n):
                j, h = half_of(n)
                dve.wait_ge(scaled, OUTS * b + n + 1)
                nc.vector.tensor_tensor(stage[:, n % SLOTS, :], stage[:, n % SLOTS, :],
                                        X[:, j, h * BANK:(h + 1) * BANK], ALU.add).then_inc(drained, 1)

            def batch(b, last):
                def make_next_zt(n):
                    if last:
                        return
                    if n == 0:
                        for a in range(QUARTERS):
                            dve.wait_ge(z_loaded[a], 16 * b + 32)
                    make_zt(b + 1, n)

                def split_next_zt(n):
                    if not last:
                        split_zt(b + 1, n)

                split_s(b, 0)
                sum_phi(b, 0)
                split_x(b, 0)
                split_x(b, 1)
                split_s(b, 1)
                sum_phi(b, 1)
                split_x(b, 2)
                split_x(b, 3)
                split_s(b, 2)
                sum_phi(b, 2)
                split_s(b, 3)
                sum_phi(b, 3)
                make_next_zt(0)
                make_next_zt(1)
                split_theta(b, 0)
                split_mirror(b, 0)
                split_mirror(b, 1)
                turn_phi_sum(b)
                split_next_zt(0)
                sum_quarters(b)
                split_next_zt(1)
                split_theta(b, 1)
                whole_t(b, 0)
                make_next_zt(2)
                split_t(b, 0)
                whole_t(b, 1)
                make_next_zt(3)
                split_t(b, 1)
                whole_t(b, 2)
                split_next_zt(2)
                make_next_zt(4)
                split_t(b, 2)
                whole_t(b, 3)
                split_t(b, 3)
                for n in (5, 6, 7):
                    split_next_zt(n - 2)
                    make_next_zt(n)
                dve.wait_ge(fold_step, FOLD_STEPS * b + QUARTERS + FOLD_STEPS)
                whole_l(b, 0)
                whole_l(b, 1)
                split_l(b, 0)
                split_l(b, 1)
                split_next_zt(6)
                split_next_zt(7)
                split_theta(b, 2)
                split_theta(b, 3)
                for n in range(OUTS):
                    add_up(b, n)

            dve.wait_ge(params_loaded, 16)
            v, root, r = (newton[:, n, :] for n in range(3))
            nc.vector.tensor_scalar(v, cols[:, VAR:VAR + CB], EPS, None, ALU.add).then_inc(var_ready, 1)
            for t, value in ((ZTH, 1.0), (ZTL, 0.0)):
                nc.vector.memset(t[:, :, :, P:BW].bitcast(f32), value)
            dve.wait_ge(rooted, 1)
            link(nc.vector.reciprocal(r, root))
            link(nc.vector.tensor_tensor(root, r, r, ALU.mult))
            link(nc.vector.tensor_tensor(root, root, v, ALU.mult))
            link(nc.vector.tensor_scalar(root, root, -0.5, 1.5, ALU.mult, ALU.add))
            link(nc.vector.tensor_tensor(r, r, root, ALU.mult))
            link(nc.vector.tensor_tensor(r, r, cols[:, GAMMA:GAMMA + CB], ALU.mult))
            link(nc.vector.tensor_tensor(shift[:, :], cols[:, W_B:W_B + CB], cols[:, MEAN:MEAN + CB], ALU.subtract))
            link(nc.vector.tensor_tensor(shift[:, :], shift[:, :], r, ALU.mult))
            link(nc.vector.tensor_tensor(shift[:, :], shift[:, :], cols[:, BETA:BETA + CB], ALU.add))
            nc.vector.tensor_scalar(scale[:, :], r, 1.0 / N, None, ALU.mult).then_inc(scales_made, 1)
            for n in range(NB + 1):
                if n < NB:
                    for a in range(QUARTERS):
                        if n == 0:
                            dve.wait_ge(z_half_loaded[a], 16)
                        if n == NB // 2:
                            dve.wait_ge(z_loaded[a], 16)
                    make_zt(0, n, first=n < RING)
                if n > 0:
                    split_zt(0, n - 1)
            for i in range(CB):
                if i == 0:
                    dve.wait_ge(drained, V_BANK)
                dve.wait_ge(v_rounded, i + 1)
                low(VL[:, i, :], bank[V_BANK + i][:, :], VH[:, i, :]).then_inc(drained, 1)
            with dve.Fori(0, B - 1) as b:
                batch(b, False)
            batch(B - 1, True)

        @block.tensor
        def _(pe):
            def product(dst, blocks, wait=None):
                for n, (stationary, moving) in enumerate(blocks):
                    if wait:
                        wait(n)
                    for q, (s, m) in enumerate(PARTS):
                        last = nc.tensor.matmul(dst, stationary(s), moving(m), start=(n == 0 and q == 0),
                                                stop=(n == len(blocks) - 1 and q == len(PARTS) - 1))
                return last

            def gram(b, i):
                pe.wait_ge(drained, reusable(b, f"S{i}"))
                for n in range(NB):
                    if i == 0:
                        pe.wait_ge(zt_split, NB * b + n + 1)
                    for q, (s, m) in enumerate(PARTS):
                        mm = nc.tensor.matmul(s_bank(i), ZT[s][:, n, i, 0:P], ZT[m][:, n, S_BLOCKS[i], :],
                                              start=(n == 0 and q == 0), stop=(n == NB - 1 and q == 2))
                mm.then_inc(filled, 1)

            def theta(b, n):
                m, h = n % IB, n // IB
                pe.wait_ge(drained, reusable(b, f"theta{n}"))

                def x_block_split(j):
                    pe.wait_ge(x_split, CB * b + j + 1)

                product(bank_of(f"theta{n}")[:, :],
                        [(lambda s, j=j: THETA_W[s][:, j, m * P:(m + 1) * P],
                          lambda q, j=j: XX[q][:, j, h * BANK:(h + 1) * BANK]) for j in range(CB)],
                        wait=x_block_split if n == 0 else None).then_inc(filled, 1)

            def mirror(b, n):
                pe.wait_ge(drained, reusable(b, f"mirror{n}"))
                pe.wait_ge(drained, done(b, f"S{MIRRORS[n][-1][0]}"))
                for q, (i, j) in enumerate(MIRRORS[n]):
                    mm = nc.tensor.transpose(bank_of(f"mirror{n}")[:, q * P:(q + 1) * P],
                                             full[:, i, j, :], ident[:, :])
                mm.then_inc(filled, 1)

            def batch(b):
                for i in range(CB):
                    gram(b, i)
                pe.wait_ge(theta_w_split, 1)
                theta(b, 0)
                mirror(b, 0)
                mirror(b, 1)
                theta(b, 1)
                pe.wait_ge(phi_w_split, 1)
                for i in range(CB):
                    if i < 2:
                        pe.wait_ge(drained, done(b, f"mirror{i}"))
                    mm = product(bank_of(f"T{i}")[:, 0:CI],
                                 [(lambda s, j=j: SS[s][:, j, i, :],
                                   lambda q, j=j: PHI_W[q][:, j, :]) for j in range(CB)])
                    mm.then_inc(filled, 1)
                pe.wait_ge(drained, reusable(b, "L1"))
                for j in range(CB):
                    pe.wait_ge(t_split, CB * b + j + 1)
                    for m in range(IB):
                        for q, (s, v) in enumerate(PARTS):
                            mm = nc.tensor.matmul(bank_of(f"L{m}")[:, :], TT[s][:, j, m * P:(m + 1) * P],
                                                  VV[v][:, j, :], start=(j == 0 and q == 0), stop=(j == CB - 1 and q == 2))
                        if j == CB - 1:
                            mm.then_inc(filled, 1)
                theta(b, 2)
                theta(b, 3)
                for n in range(OUTS):
                    pe.wait_ge(drained, reusable(b, f"out{n}"))
                    if n == 0:
                        pe.wait_ge(l_split, IB * b + IB)
                    if n == 2:
                        pe.wait_ge(drained, done(b, "theta3"))
                    j, h = half_of(n)
                    product(bank_of(f"out{n}")[:, :],
                            [(lambda s, m=m: LX[s][:, m, j * P:(j + 1) * P],
                              lambda q, m=m: THETA[q][:, m, h * BANK:(h + 1) * BANK]) for m in range(IB)]).then_inc(filled, 1)

            pe.wait_ge(ones_made, 1)
            for n in range(WARM_UP):
                mm = nc.tensor.matmul(bank[0][:, 0:P], ones[:, :], ones[:, :], start=True, stop=True)
            mm.then_inc(drained, V_BANK - 1)
            for m in range(IB):
                pe.wait_ge(slot_moved[m], 16)
                pe.wait_ge(slot_moved[IB + m], 16)
                for i in range(CB):
                    mm = nc.tensor.matmul(bank[V_BANK + i][:, :], gw_raw[:, m, i * P:(i + 1) * P], wwT_raw[:, m, :],
                                          start=(m == 0), stop=(m == IB - 1))
                    if m == IB - 1:
                        mm.then_inc(filled, 1)
            pe.wait_ge(h_parts_step, IB + 1)
            nc.tensor.matmul(bank[V_BANK - 1][:, :], ones[:, :], h_parts[:, 0, :], start=True, stop=True
                             ).then_inc(filled, V_BANK)
            pe.wait_ge(ident_made, 1)
            with pe.Fori(0, B - 1) as b:
                batch(b)
            batch(B - 1)


def kernel(**inputs):
    import numpy as np
    import concourse.bacc as bacc
    from concourse.bass_utils import run_bass_kernel_spmd

    def of(name):
        return np.ascontiguousarray(inputs[name])

    def blocks(name):
        return of(f"L0_xattn_{name}").reshape(-1, P).T

    x = of("x")
    columns = np.concatenate([blocks(n) for n in
                              ("theta_b", "phi_b", "g_b", "w_b", "bn_mean", "bn_beta", "bn_gamma", "bn_var")], axis=1)
    rows = of("L0_xattn_phi_b")[None, :]
    arrays = {
        "x": x,
        "ctx": of("ctx_2048"),
        "theta_wT": np.ascontiguousarray(of("L0_xattn_theta_w").T),
        "phi_wT": np.ascontiguousarray(of("L0_xattn_phi_w").T),
        "g_w": of("L0_xattn_g_w"),
        "w_wT": np.ascontiguousarray(of("L0_xattn_w_w").T),
        "columns": np.ascontiguousarray(columns),
        "rows": np.ascontiguousarray(rows),
    }
    nc = bacc.Bacc("TRN2", target_bir_lowering=False, num_devices=1)
    args = [nc.dram_tensor(f"{name}_dram", a.shape, mybir.dt.from_np(a.dtype), kind="ExternalInput").ap()
            for name, a in arrays.items()]
    args.append(nc.dram_tensor("out_dram", x.shape, mybir.dt.from_np(x.dtype), kind="ExternalOutput").ap())
    xattn(nc, *args)
    r = run_bass_kernel_spmd(nc, [{f"{name}_dram": a for name, a in arrays.items()}], core_ids=[0])
    return r.results[0]["out_dram"]
```
